# Optimizing a Trainium2 kernel written in Bass

```python
import numpy as np
import jax
import jax.numpy as jnp

def _softmax(x, axis=-1):
    return jax.nn.softmax(x, axis=axis)

def _gelu(x):
    return jax.nn.gelu(x, approximate=True)

def _silu(x):
    return jax.nn.silu(x)

def _sigmoid(x):
    return jax.nn.sigmoid(x)

def _layernorm(x, axis=-1, eps=1e-05):
    m = jnp.mean(x, axis=axis, keepdims=True)
    v = jnp.var(x, axis=axis, keepdims=True)
    return (x - m) / jnp.sqrt(v + eps)

def _scatter_add(tgt, idx, src, axis=0):
    return tgt.at[idx].add(src)

def _segment_sum(src, seg, n):
    return jax.ops.segment_sum(src, seg, n)
kernel_name = 'mk_seq_postln_d1_jaxref_r4_d4c86f'

def setup_inputs(seed: int=0):
    np.random.seed(seed)
    _w = jnp.asarray

    def _L0_attn_setup():
        import jax, jax.numpy as jnp
        import numpy as np
        B, T, D = (2, 512, 1024)
        H = 32
        HKV = 1
        HD = D // H
        key = jax.random.key(seed)
        ks = jax.random.split(key, 9)
        s = lambda fan_in: 1.0 / np.sqrt(fan_in)
        return {'x': jax.random.normal(ks[0], (B, T, D), dtype=jnp.float32), 'wq_w': jax.random.normal(ks[1], (H * HD, D), dtype=jnp.float32) * s(D), 'wq_b': jax.random.normal(ks[2], (H * HD,), dtype=jnp.float32) * 0.02, 'wk_w': jax.random.normal(ks[3], (HKV * HD, D), dtype=jnp.float32) * s(D), 'wk_b': jax.random.normal(ks[4], (HKV * HD,), dtype=jnp.float32) * 0.02, 'wv_w': jax.random.normal(ks[5], (HKV * HD, D), dtype=jnp.float32) * s(D), 'wv_b': jax.random.normal(ks[6], (HKV * HD,), dtype=jnp.float32) * 0.02, 'wo_w': jax.random.normal(ks[7], (D, H * HD), dtype=jnp.float32) * s(H * HD), 'wo_b': jax.random.normal(ks[8], (D,), dtype=jnp.float32) * 0.02}
    _L0_attn_in = _L0_attn_setup()

    def _L0_ffn_setup():
        import jax, jax.numpy as jnp
        import numpy as np
        FP8_MAX = 448.0
        EPS = 1e-12
        key = jax.random.key(seed)
        kx, kw = jax.random.split(key)
        x = jax.random.normal(kx, (8, 512, 1024), dtype=jnp.float32)
        weight = jax.random.normal(kw, (1024, 1024), dtype=jnp.float32) * 0.02
        return {'x': x, 'weight': weight}
    _L0_ffn_in = _L0_ffn_setup()
    _d = {'L0_attn_x': _L0_attn_in['x'], 'L0_attn_wq_w': _L0_attn_in['wq_w'], 'L0_attn_wq_b': _L0_attn_in['wq_b'], 'L0_attn_wk_w': _L0_attn_in['wk_w'], 'L0_attn_wk_b': _L0_attn_in['wk_b'], 'L0_attn_wv_w': _L0_attn_in['wv_w'], 'L0_attn_wv_b': _L0_attn_in['wv_b'], 'L0_attn_wo_w': _L0_attn_in['wo_w'], 'L0_attn_wo_b': _L0_attn_in['wo_b'], 'L0_ffn_weight': _L0_ffn_in['weight']}
    _x0 = _d['L0_attn_x']
    _d['L0_attn_x'] = jax.random.normal(jax.random.fold_in(jax.random.key(seed), 1), (2, 2048, 1024), dtype=_x0.dtype)
    del _x0
    return _d

def reference(L0_attn_x, L0_attn_wq_w, L0_attn_wq_b, L0_attn_wk_w, L0_attn_wk_b, L0_attn_wv_w, L0_attn_wv_b, L0_attn_wo_w, L0_attn_wo_b, L0_ffn_weight):

    def _L0_attn_ref(x, wq_w, wq_b, wk_w, wk_b, wv_w, wv_b, wo_w, wo_b):
        import jax, jax.numpy as jnp
        import numpy as np
        B, T, D = (2, 512, 1024)
        H = 32
        HKV = 1
        HD = D // H
        b, t, d = x.shape
        q = (x @ wq_w.T + wq_b).reshape(b, t, H, HD)
        k = (x @ wk_w.T + wk_b).reshape(b, t, HKV, HD)
        v = (x @ wv_w.T + wv_b).reshape(b, t, HKV, HD)
        k1 = k[:, :, 0, :]
        v1 = v[:, :, 0, :]
        scores = jnp.einsum('bqhd,bkd->bhqk', q, k1) / jnp.sqrt(jnp.float32(HD))
        causal = jnp.tril(jnp.ones((t, t), dtype=bool))
        scores = jnp.where(causal, scores, -jnp.inf)
        weights = jax.nn.softmax(scores, axis=-1)
        attn = jnp.einsum('bhqk,bkd->bqhd', weights, v1)
        attn = attn.reshape(b, t, H * HD)
        return attn @ wo_w.T + wo_b

    def _L0_ffn_ref(x, weight):
        import jax, jax.numpy as jnp
        import numpy as np
        FP8_MAX = 448.0
        EPS = 1e-12
        B, S, K = x.shape
        N = weight.shape[1]
        x2 = x.reshape(-1, K)
        x_scale = FP8_MAX / jnp.maximum(jnp.max(jnp.abs(x2)), EPS)
        w_scale = FP8_MAX / jnp.maximum(jnp.max(jnp.abs(weight)), EPS)
        x_sim = jnp.clip(x2 * x_scale, -FP8_MAX, FP8_MAX)
        w_sim = jnp.clip(weight * w_scale, -FP8_MAX, FP8_MAX)
        out = x_sim @ w_sim * (1.0 / (x_scale * w_scale))
        return out.reshape(B, S, N)
    x = L0_attn_x
    x = _layernorm(x + _L0_attn_ref(x, L0_attn_wq_w, L0_attn_wq_b, L0_attn_wk_w, L0_attn_wk_b, L0_attn_wv_w, L0_attn_wv_b, L0_attn_wo_w, L0_attn_wo_b), axis=-1)
    x = _layernorm(x + _L0_ffn_ref(x, L0_ffn_weight), axis=-1)
    return x

_drawn_inputs = setup_inputs


def setup_inputs(seed=0):
    import zlib

    import numpy as np

    out = dict(_drawn_inputs(seed))
    spreads = {}
    factors = {'L0_attn_wq_b': 31.818, 'L0_attn_wk_b': 64.0, 'L0_attn_wo_b': 3.015}
    for name, (base, spread) in spreads.items():
        noise = np.random.default_rng([zlib.crc32(name.encode()), seed]).standard_normal(out[name].shape)
        drawn = base * np.exp(spread * noise) if base else spread * noise
        out[name] = jnp.asarray(drawn.astype(out[name].dtype))
    for name, factor in factors.items():
        out[name] = (out[name] * factor).astype(out[name].dtype)
    return out
```

```python
from contextlib import ExitStack

import concourse.bass as bass
from concourse import mybir

F32 = mybir.dt.float32
F32R = mybir.dt.float32r
BF16 = mybir.dt.bfloat16
I32 = mybir.dt.int32
ALU = mybir.AluOpType
ACT = mybir.ActivationFunctionType
AX = mybir.AxisListType
RMAX = bass.bass_isa.ReduceOp.max

P = 128
FP8_MAX = 448.0
SCALE_EPS = 1e-12
LN_EPS = 1e-5
EXP_SAFE = 40.0
MASKED = -3.0e38


def build(nc, x_t, x, w_qkv, b_qkv, w_o, b_o, w_f, out, B, T, H):
    D = x.shape[1]
    HD = D // H
    KT = D // P
    NB = 512
    TB = B * T // NB
    JB = T // NB
    QT = NB // P
    TT = T // P
    TILES = B * TT
    HG = P // HD
    G = H // HG
    MT = G + 1
    NH = D // 512
    SR = 3 * HD
    SM = SR + 2
    SCALE = float(HD) ** -0.5
    SAFE_NORMS = (EXP_SAFE / SCALE) ** 2
    RING = 3
    SLOTS = QT
    LN = 7
    LN2 = 6
    assert HG == 4 and MT % RING == 0 and TB % 2 == 0 and G % 2 == 0 and TILES % 4 == 0

    q_hi_d = nc.dram_tensor("q_hi_d", (TB, H * HD, NB), F32).ap()
    q_lo_d = nc.dram_tensor("q_lo_d", (TB, H * HD, NB), F32).ap()
    k_st_d = nc.dram_tensor("k_st_d", (TB, SR, NB), F32).ap()
    v_d = nc.dram_tensor("v_d", (TB, P, QT, HD), F32).ap()
    max_d = nc.dram_tensor("max_d", (2, TB, H, NB), F32).ap()
    x1_d = nc.dram_tensor("x1_d", (TILES, P, D), F32).ap()
    x_tiles = x.rearrange("(n p) d -> n p d", p=P)
    out_tiles = out.rearrange("(n p) d -> n p d", p=P)

    ctx = ExitStack()

    def sem(name):
        return ctx.enter_context(nc.semaphore(name))

    with ctx:
        def sb(name, shape, dt=F32, stack=ctx):
            return stack.enter_context(nc.sbuf_tensor(name, shape, dt))

        ident = sb("ident", [P, P])
        ident_bf = sb("ident_bf", [P, P], BF16)
        mask_bf = sb("mask_bf", [P, P], BF16)
        amax_x = sb("amax_x", [P, TILES])
        small = sb("small", [P, 32])
        exponent = sb("exponent", [P, 1])
        flag = sb("flag", [P, 1], I32)

        with ExitStack() as s:
            w_hi = sb("w_hi", [P, KT, MT * P], F32R, s)
            w_lo = sb("w_lo", [P, KT, MT * P], F32R, s)
            xt_raw = sb("xt_raw", [P, KT, NB], F32, s)
            xt_hi = sb("xt_hi", [P, 2, KT, NB], F32R, s)
            xt_lo = sb("xt_lo", [P, 2, KT, NB], F32R, s)
            bias = sb("bias", [P, MT], F32, s)
            head_sum = sb("head_sum", [P, P], F32R, s)
            raw = sb("raw", [P, RING, NB], F32, s)
            sq = sb("sq", [P, RING, NB], F32R, s)
            part_hi = sb("part_hi", [P, RING, NB], F32R, s)
            part_lo = sb("part_lo", [P, RING, NB], F32R, s)
            v_t = sb("v_t", [P, QT, HD], F32, s)
            norms = sb("norms", [P, TB, MT], F32, s)
            zeros = sb("zeros", [P, NB], F32R, s)
            w_stage = xt_raw[:].rearrange("p k n -> p (k n)")[:, 0:2 * MT * P].rearrange("p (s n) -> p s n", s=2)

        with ExitStack() as s:
            q_m = sb("q_m", [SR, 2, T], F32R, s)
            k_m = sb("k_m", [SR, T], F32R, s)
            row_max = sb("row_max", [P, TT], F32, s)
            max_hi = sb("max_hi", [TT, P], F32R, s)
            max_lo = sb("max_lo", [TT, P], F32R, s)

        with ExitStack() as s:
            wo_hi = sb("wo_hi", [P, KT, D], F32R, s)
            wo_lo = sb("wo_lo", [P, KT, D], F32R, s)
            bo = sb("bo", [P, D], F32, s)
            k_st = sb("k_st", [SM, T], F32R, s)
            v_sb = sb("v_sb", [P, TT, HD], F32, s)
            q_st = sb("q_st", [SM, 2, HG, NB], F32R, s)
            prob = sb("prob", [P, SLOTS, HG, NB], F32, s)
            acc = sb("acc", [P, 2, HG, NB], F32, s)
            ones = sb("ones", [P, HD], F32, s)
            r_den = sb("r_den", [P, NB], F32, s)
            att = sb("att", [P, 2, NB], F32, s)
            att_hi = sb("att_hi", [P, G, NB], F32R, s)
            att_lo = sb("att_lo", [P, G, NB], F32R, s)
            x_res = sb("x_res", [P, 2, D], F32, s)
            y1 = sb("y1", [P, 2, D], F32, s)
            stats = sb("stats", [P, 2, NH, 6], F32, s)
            moments = sb("moments", [P, 2, 4], F32, s)
            wo_stage = acc[:].rearrange("p a h n -> p a (h n)")[:, :, 0:D]

        with ExitStack() as s:
            wf = sb("wf", [P, KT, D], F32, s)
            wf_hi = sb("wf_hi", [P, KT, D], F32R, s)
            wf_lo = sb("wf_lo", [P, KT, D], F32R, s)
            x1 = sb("x1", [P, 4, D], F32, s)
            x_sim = sb("x_sim", [P, 2, D], F32, s)
            xs_hi = sb("xs_hi", [P, 2, KT, P], F32R, s)
            xs_lo = sb("xs_lo", [P, 2, KT, P], F32R, s)
            y2 = sb("y2", [P, 2, D], F32, s)
            stats2 = sb("stats2", [P, 2, NH, 6], F32, s)
            moments2 = sb("moments2", [P, 2, 4], F32, s)

        bank = ctx.enter_context(nc.psum_tensor("bank", [P, 8, 512], F32))

        consts = sem("consts")
        w_in = [sem("w_in0"), sem("w_in1")]
        w_hi_cut, w_cut = sem("w_hi_cut"), sem("w_cut")
        passed = sem("passed")
        b_in = sem("b_in")
        zeros_sent = sem("zeros_sent")
        xt_in = sem("xt_in")
        xt_hi_cut, xt_cut = sem("xt_hi_cut"), sem("xt_cut")
        qkv_done = sem("qkv_done")
        raw_ready = sem("raw_ready")
        sq_ready = sem("sq_ready")
        norm_done = sem("norm_done")
        norm_read = sem("norm_read")
        hi_cut = sem("hi_cut")
        lo_cut = sem("lo_cut")
        part_sent = [sem(f"part_sent{i}") for i in range(RING)]
        v_turned = sem("v_turned")
        v_ready = sem("v_ready")
        v_sent = sem("v_sent")
        bound_steps = sem("bound_steps")
        bound_all = sem("bound_all")
        flag_ready = sem("flag_ready")
        project_over = sem("project_over")

        m_k_in = sem("m_k_in")
        m_q_in = [sem("m_q_in0"), sem("m_q_in1")]
        m_s_done = sem("m_s_done")
        m_s_read = sem("m_s_read")
        m_turned = sem("m_turned")
        m_hi_cut, m_lo_cut = sem("m_hi_cut"), sem("m_lo_cut")
        m_sent = sem("m_sent")
        attend_go = sem("attend_go")

        wo_in = [sem("wo_in0"), sem("wo_in1")]
        wo_hi_cut, wo_cut = sem("wo_hi_cut"), sem("wo_cut")
        bo_in = sem("bo_in")
        fixed = sem("fixed")
        kv_in = sem("kv_in")
        q_in = sem("q_in")
        s_done = sem("s_done")
        p_done = sem("p_done")
        masked = sem("masked")
        pv_done = sem("pv_done")
        acc_done = sem("acc_done")
        den_done = sem("den_done")
        den_read = sem("den_read")
        att_ready = sem("att_ready")
        att_hi_cut = sem("att_hi_cut")
        att_cut = sem("att_cut")
        y_done = sem("y_done")
        y_read = sem("y_read")
        res_in = [sem("res_in0"), sem("res_in1")]
        res_ready = sem("res_ready")
        ln1 = sem("ln1")
        x1_sent = [sem("x1_sent0"), sem("x1_sent1")]

        wf_in = sem("wf_in")
        wf_steps = sem("wf_steps")
        g_all = sem("g_all")
        x1_in = [sem(f"x1_in{i}") for i in range(4)]
        sim_ready = sem("sim_ready")
        t_done = sem("t_done")
        t_hi = sem("t_hi")
        t_lo = sem("t_lo")
        f_done = sem("f_done")
        f_read = sem("f_read")
        ln2 = sem("ln2")
        y_sent = [sem("y_sent0"), sem("y_sent1")]

        BLOCK_GROUPS = G
        SEQ_STEPS = G * QT * JB * (JB + 1) // 2

        def group(b, j, gp, r):
            return b * (JB * G) + (j * G + r) + gp * 2

        def step(b, j, gp, r):
            n = QT * (j + 1)
            return b * SEQ_STEPS + (G * QT * j * (j + 1) // 2 + r * n) + gp * (2 * n)

        def first_query(j, t):
            return P * max(0, t - QT * j)

        def three_products(dst, a_hi, a_lo, c_hi, c_lo, first, last):
            nc.tensor.matmul(dst, a_hi, c_hi, start=first, stop=False)
            nc.tensor.matmul(dst, a_lo, c_hi, start=False, stop=False)
            return nc.tensor.matmul(dst, a_hi, c_lo, start=False, stop=last)

        def wait_apart(eng, semaphore, value):
            eng.wait_ge(semaphore, value)
            eng.sem_inc(passed, 1)

        block = ctx.enter_context(nc.Block())

        @block.sync
        def _(sp):
            sp.dma_start(bias[:], b_qkv).then_inc(b_in, 16)
            for k in range(KT):
                if k >= 2:
                    sp.wait_ge(w_cut, k - 1)
                sp.dma_start(w_stage[:, k % 2], w_qkv[:, k]).then_inc(w_in[k % 2], 16)
            sp.wait_ge(w_cut, KT)
            with sp.Fori(0, TB) as tb:
                sp.wait_ge(xt_cut, tb + 1)
                sp.dma_start(xt_raw[:], x_t[bass.ds(tb, 1)].rearrange("a p k n -> p (a k) n")).then_inc(xt_in, 16)
            for i in range(RING):
                sp.wait_ge(part_sent[i], 32 * (TB * MT // RING + 1))
            sp.wait_ge(v_sent, 16 * (TB + 1))
            sp.wait_ge(zeros_sent, 32 * H * TB // P)
            sp.wait_ge(flag_ready, 1)
            sp.sem_inc(project_over, 1)

            needed = sp.value_load(flag[0:1, 0:1], min_val=0, max_val=1)
            with sp.If(needed == 1):
                q_hi_m = q_hi_d.rearrange("t (h p) n -> h p t n", p=HD)
                q_lo_m = q_lo_d.rearrange("t (h p) n -> h p t n", p=HD)
                with sp.Fori(0, B) as b:
                    blocks = bass.ds(b * JB, JB)
                    sp.wait_ge(m_turned, b * H + 2)
                    sp.dma_start(k_m[:].bitcast(F32).rearrange("r (t n) -> r t n", n=NB), k_st_d[blocks].rearrange("t r n -> r t n")).then_inc(m_k_in, 16)
                    with sp.Fori(0, H // 2) as hp:
                        for r in range(2):
                            n = b * H + r + hp * 2
                            head = bass.ds(hp * 2 + r, 1)
                            sp.wait_ge(m_turned, n + 1)
                            for rows, src in ((0, q_hi_m), (HD, q_lo_m), (2 * HD, q_hi_m)):
                                sp.dma_start(q_m[rows:rows + HD, r].bitcast(F32).rearrange("p (t n) -> p t n", n=NB),
                                             src[head, :, blocks].rearrange("a p t n -> (a p) t n")).then_inc(m_q_in[r], 16)
                sp.wait_ge(m_sent, 32 * JB * (B * H + 1))
            sp.sem_inc(attend_go, 1)

            sp.dma_start(bo[:], b_o).then_inc(bo_in, 16)
            for k in range(KT):
                if k >= 2:
                    sp.wait_ge(wo_cut, k - 1)
                sp.dma_start(wo_stage[:, k % 2], w_o[:, k]).then_inc(wo_in[k % 2], 16)
            q_hi_h = q_hi_d.rearrange("t (h p) n -> (t h) p n", p=HD)
            q_lo_h = q_lo_d.rearrange("t (h p) n -> (t h) p n", p=HD)
            max_h = max_d.rearrange("c t h n -> c (t h) n")
            with sp.Fori(0, B) as b:
                sp.wait_ge(y_done, b * (JB * QT) + QT)
                blocks = bass.ds(b * JB, JB)
                sp.dma_start(k_st[0:SR].bitcast(F32).rearrange("r (t n) -> r t n", n=NB), k_st_d[blocks].rearrange("t r n -> r t n")).then_inc(kv_in, 16)
                sp.dma_start(v_sb[:].rearrange("p (t q) d -> p t (q d)", q=QT), v_d[blocks].rearrange("t p q d -> p t (q d)")).then_inc(kv_in, 16)
                for j in range(JB):
                    blk = b * JB + j

                    def residual(t):
                        sp.wait_ge(ln1, (blk * QT + t) * LN + 1)
                        sp.dma_start(x_res[:, t % 2], x_tiles[bass.ds(blk * QT + t, 1)].rearrange("a p d -> p (a d)")).then_inc(res_in[t % 2], 16)

                    residual(0)
                    residual(1)
                    with sp.Fori(0, G // 2) as gp:
                        for r in range(2):
                            n = group(b, j, gp, r)
                            heads = bass.ds(n * HG, HG)
                            sp.wait_ge(den_done, n + 1)
                            sp.dma_start(q_st[0:HD, r].bitcast(F32), q_hi_h[heads].rearrange("h p n -> p h n")).then_inc(q_in, 16)
                            sp.dma_start(q_st[HD:2 * HD, r].bitcast(F32), q_lo_h[heads].rearrange("h p n -> p h n")).then_inc(q_in, 16)
                            sp.dma_start(q_st[2 * HD:SR, r].bitcast(F32), q_hi_h[heads].rearrange("h p n -> p h n")).then_inc(q_in, 16)
                            sp.dma_start(q_st[SR:SM, r].bitcast(F32), max_h[:, heads]).then_inc(q_in, 16)
                            wait_apart(sp, q_in, n * 64 + 64)
                    residual(2)
                    residual(3)

            for i in range(2):
                sp.wait_ge(x1_sent[i], 16 * (TILES // 2 + 1))
            sp.wait_ge(ln1, LN * (TILES + 2))
            sp.dma_start(wf[:], w_f).then_inc(wf_in, 16)
            with sp.Fori(0, TILES // 4) as i:
                for r in range(4):
                    sp.wait_ge(f_read, i * 4 + r + 1)
                    sp.dma_start(x1[:, r], x1_d[bass.ds(i * 4 + r, 1)].rearrange("a p d -> p (a d)")).then_inc(x1_in[r], 16)
            for i in range(2):
                sp.wait_ge(y_sent[i], 16 * (TILES // 2 + 1))

        @block.gpsimd
        def _(pool):
            pool.sem_inc(xt_cut, 1)
            pool.sem_inc(att_cut, 2)
            nc.gpsimd.memset(ident[:], 0.0).then_inc(consts, 1)
            nc.gpsimd.memset(mask_bf[:], 0.0).then_inc(consts, 1)
            nc.gpsimd.memset(head_sum[:].bitcast(F32), 0.0).then_inc(consts, 1)
            nc.gpsimd.memset(zeros[:].bitcast(F32), 0.0).then_inc(consts, 1)
            nc.gpsimd.memset(exponent[:], -0.5).then_inc(consts, 1)
            pool.wait_ge(consts, 5)
            nc.gpsimd.affine_select(out=ident[:], in_=ident[:], compare_op=ALU.not_equal, fill=1.0,
                                    base=0, pattern=[[-1, P]], channel_multiplier=1).then_inc(consts, 1)
            nc.gpsimd.affine_select(out=mask_bf[:], in_=mask_bf[:], compare_op=ALU.is_ge, fill=MASKED,
                                    base=0, pattern=[[-1, P]], channel_multiplier=1).then_inc(consts, 1)
            for h in range(HG):
                pool.wait_ge(consts, 7 + h)
                nc.gpsimd.memset(head_sum[h * HD:(h + 1) * HD, h * HD:(h + 1) * HD].bitcast(F32), 1.0).then_inc(consts, 1)
            pool.wait_ge(consts, 7 + HG)
            nc.gpsimd.tensor_copy(ident_bf[:], ident[:]).then_inc(consts, 1)

            def inverse_deviation(moments, done, before):
                wait_apart(pool, done, before + (NH + 1))
                nc.gpsimd.tensor_scalar(moments[:, 1:2], moments[:, 1:2], LN_EPS, None, ALU.add).then_inc(done, 1)
                wait_apart(pool, done, before + (NH + 2))
                nc.gpsimd.tensor_tensor(moments[:, 2:3], moments[:, 1:2], exponent[:], ALU.pow).then_inc(done, 1)

            with pool.Fori(0, TB // 2) as i:
                for r in range(2):
                    tb = i * 2 + r
                    pool.wait_ge(xt_in, tb * 16 + 16)
                    wait_apart(pool, qkv_done, tb * MT + MT)
                    nc.gpsimd.tensor_copy(xt_hi[:, r], xt_raw[:]).then_inc(xt_hi_cut, 1)
                    wait_apart(pool, xt_hi_cut, tb + 1)
                    nc.gpsimd.tensor_tensor(xt_lo[:, r], xt_raw[:], xt_hi[:, r].bitcast(F32), ALU.subtract).then_inc(xt_cut, 1)
            pool.wait_ge(bound_steps, 3)
            nc.gpsimd.partition_all_reduce(small[:, 2:4], small[:, 0:2], P, RMAX).then_inc(bound_all, 1)

            pool.wait_ge(attend_go, 1)
            nc.gpsimd.memset(k_st[SR:SM].bitcast(F32), -1.0).then_inc(fixed, 1)
            pool.wait_ge(fixed, 1)
            nc.gpsimd.memset(ones[:], 1.0).then_inc(fixed, 1)
            pool.wait_ge(bo_in, 16)
            pool.wait_ge(fixed, 2)
            with pool.Fori(0, B) as b:
                for j in range(JB):
                    blk = b * JB + j

                    def residual(t):
                        pool.wait_ge(res_in[t % 2], (blk * (QT // 2) + t // 2) * 16 + 16)
                        nc.gpsimd.tensor_tensor(x_res[:, t % 2], x_res[:, t % 2], bo[:], ALU.add).then_inc(res_ready, 1)

                    residual(0)
                    residual(1)
                    with pool.Fori(0, G // 2) as gp:
                        for r in range(2):
                            n, s0 = group(b, j, gp, r), step(b, j, gp, r)
                            for i in range(QT):
                                t = QT * j + i
                                off = first_query(j, t)
                                wait_apart(pool, p_done, s0 * 2 + (2 * t + 4))
                                tri = prob[:, t % SLOTS, :, off:off + P]
                                nc.gpsimd.affine_select(out=tri, in_=tri, compare_op=ALU.is_ge, fill=0.0, base=0,
                                                        pattern=[[0, HG], [1, P]], channel_multiplier=-1).then_inc(masked, 1)
                            pool.wait_ge(att_hi_cut, n + 1)
                            g = bass.ds(gp * 2 + r, 1)
                            nc.gpsimd.tensor_tensor(att_lo[:, g].rearrange("p a n -> p (a n)"), att[:, r],
                                                    att_hi[:, g].rearrange("p a n -> p (a n)").bitcast(F32),
                                                    ALU.subtract).then_inc(att_cut, 1)
                    for t in range(QT):
                        inverse_deviation(moments[:, t % 2], ln1, (blk * QT + t) * LN + 2 * LN)
                        if t + 2 < QT:
                            residual(t + 2)

            pool.wait_ge(wf_steps, 2)
            nc.gpsimd.partition_all_reduce(small[:, 10:12], small[:, 8:10], P, RMAX).then_inc(g_all, 1)
            pool.wait_ge(wf_steps, 5)

            def clip(i, r):
                n = i * 4 + r
                pool.wait_ge(x1_in[r % 4], i * 16 + 16 * (r // 4 + 1))
                wait_apart(pool, t_done, n + 1)
                nc.gpsimd.tensor_scalar(x_sim[:, r % 2], x1[:, r % 4], small[:, 14:15], FP8_MAX, ALU.mult, ALU.min).then_inc(sim_ready, 1)
                wait_apart(pool, sim_ready, n * 2 + 1)
                nc.gpsimd.tensor_scalar(x_sim[:, r % 2], x_sim[:, r % 2], -FP8_MAX, None, ALU.max).then_inc(sim_ready, 1)

            clip(0, 0)
            clip(0, 1)
            with pool.Fori(0, TILES // 4 - 1) as i:
                for r in range(4):
                    clip(i, r + 2)
                    inverse_deviation(moments2[:, r % 2], ln2, (i * 4 + r) * LN2)
            i = TILES // 4 - 1
            for r in range(4):
                if r < 2:
                    clip(i, r + 2)
                inverse_deviation(moments2[:, r % 2], ln2, (i * 4 + r) * LN2)

        @block.scalar
        def _(act):
            act.sem_inc(sq_ready, RING)
            act.sem_inc(p_done, 2)
            for s in part_sent:
                act.sem_inc(s, 32)
            act.sem_inc(v_sent, 16)
            for s in (*x1_sent, *y_sent):
                act.sem_inc(s, 16)
            act.wait_ge(consts, 4)
            for c in range(2):
                for i in range(TB * H // P):
                    act.dma_start(max_d[c].rearrange("t h n -> (t h) n")[i * P:(i + 1) * P], zeros[:].bitcast(F32)).then_inc(zeros_sent, 16)
            act.wait_ge(b_in, 16)

            def send(tb, m):
                act.wait_ge(lo_cut, tb * MT + (m + 1 + RING))
                if m < G:
                    rows = slice(m * P, (m + 1) * P)
                    act.dma_start(q_hi_d[bass.ds(tb, 1), rows].rearrange("a p n -> p (a n)"), part_hi[:, m % RING].bitcast(F32)).then_inc(part_sent[m % RING], 16)
                    act.dma_start(q_lo_d[bass.ds(tb, 1), rows].rearrange("a p n -> p (a n)"), part_lo[:, m % RING].bitcast(F32)).then_inc(part_sent[m % RING], 16)
                else:
                    act.dma_start(k_st_d[bass.ds(tb, 1), 0:2 * HD].rearrange("a p n -> p (a n)"), part_hi[0:2 * HD, m % RING].bitcast(F32)).then_inc(part_sent[m % RING], 16)
                    act.dma_start(k_st_d[bass.ds(tb, 1), 2 * HD:SR].rearrange("a p n -> p (a n)"), part_lo[2 * HD:SR, m % RING].bitcast(F32)).then_inc(part_sent[m % RING], 16)

            with act.Fori(0, TB) as tb:
                for m in range(MT):
                    u = tb * MT + m
                    act.wait_ge(qkv_done, u + (1 + 2 * MT))
                    act.wait_ge(lo_cut, u + 1)
                    if m == G % RING:
                        act.wait_ge(v_turned, tb + 1)
                    nc.scalar.activation(raw[:, m % RING], bank[:, m % RING], ACT.Identity, bias=bias[:, m:m + 1]).then_inc(raw_ready, 1)
                    act.wait_ge(norm_done, u + 1)
                    nc.scalar.activation(sq[:, m % RING], bank[:, m % RING], ACT.Square, bias=bias[:, m:m + 1]).then_inc(sq_ready, 1)
                    if m >= 1:
                        send(tb, m - 1)
                send(tb, MT - 1)
                act.wait_ge(v_ready, tb + 2)
                act.dma_start(v_d[bass.ds(tb, 1)].rearrange("a p q d -> p (a q) d"), v_t[:]).then_inc(v_sent, 16)

            act.wait_ge(flag_ready, 1)
            needed = act.value_load(flag[0:1, 0:1], min_val=0, max_val=1)
            with act.If(needed == 1):
                act.sem_inc(m_sent, 32 * JB)
                with act.Fori(0, B) as b:
                    with act.Fori(0, H) as h:
                        act.wait_ge(m_lo_cut, b * H + h + 2)
                        for c, part in ((0, max_hi), (1, max_lo)):
                            for j in range(JB):
                                act.dma_start(max_d[c].rearrange("t h (q p) -> (t h) q p", p=P)[bass.ds(b * (JB * H) + j * H + h, 1)].rearrange("a q p -> (a q) p"),
                                              part[j * QT:(j + 1) * QT].bitcast(F32)).then_inc(m_sent, 16)

            with act.Fori(0, B) as b:
                for j in range(JB):
                    blk = b * JB + j
                    with act.Fori(0, G // 2) as gp:
                        for r in range(2):
                            s0 = step(b, j, gp, r)
                            for t in range(QT * (j + 1)):
                                off = first_query(j, t)
                                act.wait_ge(pv_done, s0 + (t + 1))
                                act.wait_ge(acc_done, s0 + (t + 1))
                                for p in range(2):
                                    act.wait_ge(s_done, s0 * 2 + (2 * t + p + 1))
                                    nc.scalar.activation(prob[:, t % SLOTS, 2 * p:2 * p + 2, off:NB], bank[:, 2 * p:2 * p + 2, off:NB],
                                                         ACT.Exp, scale=SCALE).then_inc(p_done, 1)
                    for t in range(QT):
                        tt = blk * QT + t
                        act.wait_ge(ln1, tt * LN + (2 * LN + 6))
                        act.dma_start(x1_d[bass.ds(tt, 1)].rearrange("a p d -> p (a d)"), y1[:, t % 2]).then_inc(x1_sent[t % 2], 16)

            act.wait_ge(wf_steps, 1)
            def upper(r, n):
                act.wait_ge(t_done, n + 3)
                act.wait_ge(f_done, n + 1)
                nc.scalar.activation(xs_hi[:, r % 2].rearrange("p k n -> p (k n)"),
                                     bank[:, 2 * (r % 2):2 * (r % 2) + 2].rearrange("p k n -> p (k n)"), ACT.Copy).then_inc(t_hi, 1)

            def store(r, n):
                act.wait_ge(ln2, n * LN2 + 6)
                act.dma_start(out_tiles[bass.ds(n, 1)].rearrange("a p d -> p (a d)"), y2[:, r % 2]).then_inc(y_sent[r % 2], 16)

            upper(0, 0)
            with act.Fori(0, TILES // 4 - 1) as i:
                for r in range(4):
                    upper(r + 1, i * 4 + r + 1)
                    store(r, i * 4 + r)
            i = TILES // 4 - 1
            for r in range(4):
                if r < 3:
                    upper(r + 1, i * 4 + r + 1)
                store(r, i * 4 + r)

        @block.vector
        def _(dve):
            def layer_norm(z, stats, moments, done, before):
                for h in range(NH):
                    nc.vector.bn_stats(stats[:, h], z[:, h * 512:(h + 1) * 512]).then_inc(done, 1)
                wait_apart(dve, done, before + NH)
                nc.vector.bn_aggr(moments[:, 0:2], stats[:]).then_inc(done, 1)
                dve.wait_ge(done, before + (NH + 3))
                nc.vector.tensor_scalar(z, z, moments[:, 0:1], moments[:, 2:3], ALU.subtract, ALU.mult).then_inc(done, 1)

            dve.sem_inc(norm_read, RING)
            dve.sem_inc(lo_cut, RING)
            dve.sem_inc(v_ready, 1)
            dve.sem_inc(acc_done, SLOTS)
            dve.sem_inc(den_read, 1)
            dve.sem_inc(att_ready, 2)
            dve.sem_inc(y_read, 2)
            dve.sem_inc(ln1, 2 * LN)
            dve.sem_inc(t_lo, 2)
            dve.sem_inc(f_read, 4)
            for k in range(KT):
                dve.wait_ge(w_in[k % 2], 16 * (k // 2 + 1))
                nc.vector.tensor_copy(w_hi[:, k], w_stage[:, k % 2]).then_inc(w_hi_cut, 1)
                dve.wait_ge(w_hi_cut, k + 1)
                nc.vector.tensor_tensor(w_lo[:, k], w_stage[:, k % 2], w_hi[:, k].bitcast(F32), ALU.subtract).then_inc(w_cut, 1)

            def norm(tb, m):
                dve.wait_ge(norm_done, tb * MT + (m + 1 + RING))
                nc.vector.reduce_max(norms[:, bass.ds(tb, 1), m:m + 1].rearrange("p a b -> p (a b)"), bank[:, RING + m % RING], AX.X).then_inc(norm_read, 1)

            with dve.Fori(0, TB) as tb:
                for m in range(MT):
                    u = tb * MT + m
                    dve.wait_ge(raw_ready, u + 1)
                    dve.wait_ge(part_sent[m % RING], tb * (32 * MT // RING) + 32 * (m // RING + 1))
                    nc.vector.tensor_copy(part_hi[:, m % RING], raw[:, m % RING]).then_inc(hi_cut, 1)
                    dve.wait_ge(hi_cut, u + 1)
                    nc.vector.tensor_tensor(part_lo[:, m % RING], raw[:, m % RING], part_hi[:, m % RING].bitcast(F32), ALU.subtract).then_inc(lo_cut, 1)
                    if m >= 1:
                        norm(tb, m - 1)
                norm(tb, MT - 1)
                dve.wait_ge(v_turned, tb + 2)
                dve.wait_ge(v_sent, tb * 16 + 16)
                nc.vector.tensor_copy(v_t[:], bank[:, 6].rearrange("p (q c) -> p q c", c=P)[:, :, SR:P]).then_inc(v_ready, 1)
            dve.wait_ge(norm_read, RING + TB * MT)
            nc.vector.memset(small[:, 0:2], 0.0).then_inc(bound_steps, 1)
            dve.wait_ge(bound_steps, 1)
            nc.vector.tensor_reduce(small[:, 0:1], norms[:, :, 0:G], AX.XY, ALU.max).then_inc(bound_steps, 1)
            nc.vector.tensor_reduce(small[0:HD, 1:2], norms[0:HD, :, G:MT].rearrange("p a b -> p (a b)"), AX.X, ALU.max).then_inc(bound_steps, 1)
            dve.wait_ge(bound_all, 1)
            nc.vector.tensor_tensor(small[:, 4:5], small[:, 2:3], small[:, 3:4], ALU.mult).then_inc(bound_steps, 1)
            dve.wait_ge(bound_steps, 4)
            nc.vector.tensor_scalar(flag[:], small[:, 4:5], SAFE_NORMS, None, ALU.is_gt).then_inc(flag_ready, 1)

            dve.wait_ge(flag_ready, 1)
            needed = dve.value_load(flag[0:1, 0:1], min_val=0, max_val=1)
            with dve.If(needed == 1):
                dve.sem_inc(m_s_read, 2)
                dve.sem_inc(m_lo_cut, 1)
                dve.wait_ge(project_over, 1)
                with dve.Fori(0, B) as b:
                    with dve.Fori(0, H) as h:
                        n = b * H + h
                        for q in range(TT):
                            scores = bank[:, 4 * (q % 2):4 * (q % 2) + 4].rearrange("p a n -> p (a n)")[:, 0:(q + 1) * P]
                            dve.wait_ge(m_s_done, n * TT + (q + 1))
                            nc.vector.reduce_max(row_max[:, q:q + 1], scores, AX.X).then_inc(m_s_read, 1)
                        dve.wait_ge(m_turned, n + 3)
                        dve.wait_ge(m_sent, n * (32 * JB) + 32 * JB)
                        nc.vector.tensor_copy(max_hi[:], bank[0:TT, 0, 0:P]).then_inc(m_hi_cut, 1)
                        dve.wait_ge(m_hi_cut, n + 1)
                        nc.vector.tensor_tensor(max_lo[:], bank[0:TT, 0, 0:P], max_hi[:].bitcast(F32), ALU.subtract).then_inc(m_lo_cut, 1)

            for k in range(KT):
                dve.wait_ge(wo_in[k % 2], 16 * (k // 2 + 1))
                nc.vector.tensor_copy(wo_hi[:, k], wo_stage[:, k % 2]).then_inc(wo_hi_cut, 1)
                dve.wait_ge(wo_hi_cut, k + 1)
                nc.vector.tensor_tensor(wo_lo[:, k], wo_stage[:, k % 2], wo_hi[:, k].bitcast(F32), ALU.subtract).then_inc(wo_cut, 1)
            dve.wait_ge(wo_cut, KT)

            with dve.Fori(0, B) as b:
                for j in range(JB):
                    blk = b * JB + j
                    with dve.Fori(0, G // 2) as gp:
                        for r in range(2):
                            n, s0 = group(b, j, gp, r), step(b, j, gp, r)
                            dve.wait_ge(den_done, n + 1)
                            for t in range(QT * (j + 1)):
                                off = first_query(j, t)
                                dve.wait_ge(p_done, s0 * 2 + (2 * t + 4))
                                if t >= QT * j:
                                    dve.wait_ge(masked, n * QT + (t - QT * j + 1))
                                new = prob[:, t % SLOTS, :, off:NB]
                                if t == 0:
                                    nc.vector.tensor_copy(acc[:, r], new).then_inc(acc_done, 1)
                                else:
                                    dve.wait_ge(acc_done, s0 + (t + SLOTS))
                                    nc.vector.tensor_tensor(acc[:, r, :, off:NB], acc[:, r, :, off:NB], new, ALU.add).then_inc(acc_done, 1)
                            dve.wait_ge(den_done, n + 3)
                            nc.vector.reciprocal(r_den[:], bank[:, 6]).then_inc(den_read, 1)
                            dve.wait_ge(den_read, n + 2)
                            dve.wait_ge(pv_done, s0 + (QT * (j + 1) + SLOTS))
                            dve.wait_ge(att_cut, n + 1)
                            nc.vector.tensor_tensor(att[:, r], bank[:, 4 + r], r_den[:], ALU.mult).then_inc(att_ready, 1)
                            dve.wait_ge(att_ready, n + 3)
                            dve.wait_ge(y_done, blk * QT + QT)
                            nc.vector.tensor_copy(att_hi[:, bass.ds(gp * 2 + r, 1)].rearrange("p a n -> p (a n)"), att[:, r]).then_inc(att_hi_cut, 1)

                    for t in range(QT):
                        s, tt = t % 2, blk * QT + t
                        z = y1[:, s]
                        steps = tt * LN + 2 * LN
                        dve.wait_ge(y_done, tt + (1 + QT))
                        dve.wait_ge(res_ready, tt + 1)
                        dve.wait_ge(x1_sent[s], (blk * (QT // 2) + t // 2) * 16 + 16)
                        nc.vector.tensor_tensor(z, bank[:, 2 * s:2 * s + NH].rearrange("p a n -> p (a n)"), x_res[:, s], ALU.add).then_inc(y_read, 1)
                        dve.wait_ge(y_read, tt + 3)
                        layer_norm(z, stats[:, s], moments[:, s], ln1, steps)
                        dve.wait_ge(ln1, steps + 6)
                        nc.vector.tensor_reduce(amax_x[:, bass.ds(tt, 1)], z, AX.X, ALU.max, apply_absolute_value=True).then_inc(ln1, 1)

            dve.wait_ge(wf_in, 16)
            dve.wait_ge(ln1, LN * (TILES + 2))
            nc.vector.tensor_reduce(small[:, 8:9], amax_x[:], AX.X, ALU.max).then_inc(wf_steps, 1)
            nc.vector.tensor_reduce(small[:, 9:10], wf[:].rearrange("p k n -> p (k n)"), AX.X, ALU.max, apply_absolute_value=True).then_inc(wf_steps, 1)
            dve.wait_ge(g_all, 1)
            nc.vector.tensor_scalar(small[:, 12:14], small[:, 10:12], SCALE_EPS, None, ALU.max).then_inc(wf_steps, 1)
            dve.wait_ge(wf_steps, 3)
            nc.vector.reciprocal(small[:, 16:18], small[:, 12:14]).then_inc(wf_steps, 1)
            dve.wait_ge(wf_steps, 4)
            nc.vector.tensor_scalar(small[:, 14:16], small[:, 16:18], FP8_MAX, None, ALU.mult).then_inc(wf_steps, 1)
            dve.wait_ge(wf_steps, 5)
            nc.vector.tensor_tensor(small[:, 18:19], small[:, 14:15], small[:, 15:16], ALU.mult).then_inc(wf_steps, 1)
            dve.wait_ge(wf_steps, 6)
            nc.vector.reciprocal(small[:, 19:20], small[:, 18:19]).then_inc(wf_steps, 1)
            nc.vector.tensor_scalar(wf[:], wf[:], small[:, 15:16], FP8_MAX, ALU.mult, ALU.min).then_inc(wf_steps, 1)
            dve.wait_ge(wf_steps, 8)
            nc.vector.tensor_scalar(wf[:], wf[:], -FP8_MAX, None, ALU.max).then_inc(wf_steps, 1)
            dve.wait_ge(wf_steps, 9)
            nc.vector.tensor_copy(wf_hi[:], wf[:]).then_inc(wf_steps, 1)
            dve.wait_ge(wf_steps, 10)
            nc.vector.tensor_tensor(wf_lo[:], wf[:], wf_hi[:].bitcast(F32), ALU.subtract).then_inc(wf_steps, 1)

            def lower(r, n):
                dve.wait_ge(t_hi, n + 1)
                dve.wait_ge(f_done, n + 1)
                nc.vector.tensor_tensor(xs_lo[:, r % 2].rearrange("p k n -> p (k n)"),
                                        bank[:, 2 * (r % 2):2 * (r % 2) + 2].rearrange("p k n -> p (k n)"),
                                        xs_hi[:, r % 2].rearrange("p k n -> p (k n)").bitcast(F32), ALU.subtract).then_inc(t_lo, 1)

            def finish(i, r, n):
                s = r % 2
                z = y2[:, s]
                dve.wait_ge(f_done, n + 3)
                dve.wait_ge(y_sent[s], i * 32 + 16 * (r // 2 + 1))
                nc.vector.scalar_tensor_tensor(out=z, in0=bank[:, 4 + 2 * s:4 + 2 * s + NH].rearrange("p a n -> p (a n)"), scalar=small[:, 19:20],
                                               in1=x1[:, r], op0=ALU.mult, op1=ALU.add).then_inc(f_read, 1)
                dve.wait_ge(f_read, n + 5)
                layer_norm(z, stats2[:, s], moments2[:, s], ln2, n * LN2)

            lower(0, 0)
            with dve.Fori(0, TILES // 4 - 1) as i:
                for r in range(4):
                    lower(r + 1, i * 4 + r + 1)
                    finish(i, r, i * 4 + r)
            i = TILES // 4 - 1
            for r in range(4):
                if r < 3:
                    lower(r + 1, i * 4 + r + 1)
                finish(i, r, i * 4 + r)

        @block.tensor
        def _(pe):
            pe.sem_inc(qkv_done, 2 * MT)
            pe.sem_inc(norm_done, RING)
            pe.sem_inc(y_done, QT)
            pe.sem_inc(v_turned, 1)
            pe.sem_inc(pv_done, SLOTS)
            pe.sem_inc(den_done, 2)
            pe.sem_inc(t_done, 2)
            pe.sem_inc(f_done, 2)
            pe.wait_ge(consts, 8 + HG)
            pe.wait_ge(w_cut, KT)

            def norm(tb, m):
                pe.wait_ge(sq_ready, tb * MT + (m + 1 + RING))
                pe.wait_ge(norm_read, tb * MT + (m + 1))
                nc.tensor.matmul(bank[:, RING + m % RING], head_sum[:], sq[:, m % RING], start=True, stop=True).then_inc(norm_done, 1)

            with pe.Fori(0, TB // 2) as i:
                for r in range(2):
                    tb = i * 2 + r
                    pe.wait_ge(xt_cut, tb + 2)
                    for m in range(MT):
                        pe.wait_ge(sq_ready, tb * MT + (m + 1))
                        cols = slice(m * P, (m + 1) * P)
                        for k in range(KT):
                            last = three_products(bank[:, m % RING], w_hi[:, k, cols], w_lo[:, k, cols], xt_hi[:, r, k], xt_lo[:, r, k], k == 0, k == KT - 1)
                        last.then_inc(qkv_done, 1)
                        if m >= 1:
                            norm(tb, m - 1)
                    norm(tb, MT - 1)
                    pe.wait_ge(raw_ready, tb * MT + MT)
                    pe.wait_ge(v_ready, tb + 1)
                    for q in range(QT):
                        last = nc.tensor.transpose(bank[:, 6, q * P:(q + 1) * P], raw[:, G % RING, q * P:(q + 1) * P], ident[:])
                    last.then_inc(v_turned, 1)

            pe.wait_ge(flag_ready, 1)
            needed = pe.value_load(flag[0:1, 0:1], min_val=0, max_val=1)
            with pe.If(needed == 1):
                pe.sem_inc(m_turned, 2)
                with pe.Fori(0, B) as b:
                    wait_apart(pe, m_k_in, b * 16 + 16)
                    with pe.Fori(0, H // 2) as hp:
                        for r in range(2):
                            n = b * H + r + hp * 2
                            pe.wait_ge(m_q_in[r], b * (48 * H // 2) + hp * 48 + 48)
                            for q in range(TT):
                                pe.wait_ge(m_s_read, n * TT + (q + 1))
                                if q == 0:
                                    pe.wait_ge(m_lo_cut, n + 1)
                                queries = q_m[:, r, q * P:(q + 1) * P]
                                for c in range(q // 4 + 1):
                                    own = c == q // 4
                                    width = (q % 4 + 1) * P if own else 512
                                    dst = bank[:, 4 * (q % 2) + c]
                                    nc.tensor.matmul(dst[:, 0:width], queries, k_m[:, c * 512:c * 512 + width], start=True, stop=not own)
                                    if own:
                                        last = nc.tensor.matmul(dst[:, width - P:width], ident_bf[:], mask_bf[:], start=False, stop=True)
                                last.then_inc(m_s_done, 1)
                            pe.wait_ge(m_s_read, n * TT + (TT + 2))
                            nc.tensor.transpose(bank[0:TT, 0, 0:P], row_max[:], ident[:]).then_inc(m_turned, 1)

            pe.wait_ge(fixed, 2)
            pe.wait_ge(wo_cut, KT)
            with pe.Fori(0, B) as b:
                wait_apart(pe, kv_in, b * 32 + 32)
                for j in range(JB):
                    blk = b * JB + j
                    NT = QT * (j + 1)
                    with pe.Fori(0, G // 2) as gp:
                        for r in range(2):
                            n, s0 = group(b, j, gp, r), step(b, j, gp, r)
                            if r == 0:
                                pe.wait_ge(y_read, blk * QT + 2)
                            pe.wait_ge(q_in, n * 64 + 64)

                            def scores(t):
                                off = first_query(j, t)
                                for p in range(2):
                                    pe.wait_ge(p_done, s0 * 2 + (2 * t + p + 1))
                                    for h in (2 * p, 2 * p + 1):
                                        last = nc.tensor.matmul(bank[:, h, off:NB], k_st[:, t * P:(t + 1) * P], q_st[:, r, h, off:NB], start=True, stop=True)
                                    last.then_inc(s_done, 1)

                            scores(0)
                            pe.wait_ge(att_ready, n + 1)
                            for t in range(NT):
                                if t + 1 < NT:
                                    scores(t + 1)
                                off = first_query(j, t)
                                pe.wait_ge(p_done, s0 * 2 + (2 * t + 4))
                                if t >= QT * j:
                                    pe.wait_ge(masked, n * QT + (t - QT * j + 1))
                                for h in range(HG):
                                    last = nc.tensor.matmul(bank[h * HD:(h + 1) * HD, 4 + r, off:NB], v_sb[:, t], prob[:, t % SLOTS, h, off:NB],
                                                            start=(t == 0), stop=(t == NT - 1), skip_group_check=True)
                                last.then_inc(pv_done, 1)
                            pe.wait_ge(acc_done, s0 + (NT + SLOTS))
                            pe.wait_ge(den_read, n + 1)
                            for h in range(HG):
                                last = nc.tensor.matmul(bank[h * HD:(h + 1) * HD, 6], ones[:], acc[:, r, h], start=True, stop=True)
                            last.then_inc(den_done, 1)
                    pe.wait_ge(att_cut, blk * G + (G + 2))
                    for t in range(QT):
                        pe.wait_ge(y_read, blk * QT + (t + 1))
                        rows = slice(t * P, (t + 1) * P)
                        for h in range(NH):
                            cols = slice(h * 512, (h + 1) * 512)
                            for k in range(KT):
                                last = three_products(bank[:, 2 * (t % 2) + h], att_hi[:, k, rows], att_lo[:, k, rows], wo_hi[:, k, cols], wo_lo[:, k, cols], k == 0, k == KT - 1)
                        last.then_inc(y_done, 1)

            def turn(r, n):
                pe.wait_ge(sim_ready, n * 2 + 2)
                pe.wait_ge(t_lo, n + 1)
                for k in range(KT):
                    last = nc.tensor.transpose(bank[:, 2 * (r % 2) + k // 4, (k % 4) * P:(k % 4 + 1) * P], x_sim[:, r % 2, k * P:(k + 1) * P], ident[:])
                last.then_inc(t_done, 1)

            def product(r, n):
                pe.wait_ge(t_lo, n + 3)
                pe.wait_ge(f_read, n + 3)
                for h in range(NH):
                    cols = slice(h * 512, (h + 1) * 512)
                    for k in range(KT):
                        last = three_products(bank[:, 4 + 2 * (r % 2) + h], xs_hi[:, r % 2, k], xs_lo[:, r % 2, k], wf_hi[:, k, cols], wf_lo[:, k, cols], k == 0, k == KT - 1)
                last.then_inc(f_done, 1)

            pe.wait_ge(y_read, TILES + 2)
            turn(0, 0)
            pe.wait_ge(wf_steps, 11)
            with pe.Fori(0, TILES // 4 - 1) as i:
                for r in range(4):
                    turn(r + 1, i * 4 + r + 1)
                    product(r, i * 4 + r)
            i = TILES // 4 - 1
            for r in range(4):
                if r < 3:
                    turn(r + 1, i * 4 + r + 1)
                product(r, i * 4 + r)

    return nc


HEADS = 32


def kernel(L0_attn_x, L0_attn_wq_w, L0_attn_wq_b, L0_attn_wk_w, L0_attn_wk_b, L0_attn_wv_w, L0_attn_wv_b,
           L0_attn_wo_w, L0_attn_wo_b, L0_ffn_weight):
    import numpy as np
    import concourse.bacc as bacc
    from concourse.bass_utils import run_bass_kernel_spmd

    x = np.ascontiguousarray(L0_attn_x)
    B, T, D = x.shape
    kt = D // P

    def by_partition(w):
        return np.ascontiguousarray(w.reshape(kt, P, -1).transpose(1, 0, 2))

    flat = x.reshape(B * T, D)
    blocks = flat.reshape(-1, 512, kt, P).transpose(0, 3, 2, 1)
    w_qkv = np.concatenate([np.asarray(w) for w in (L0_attn_wq_w, L0_attn_wk_w, L0_attn_wk_w, L0_attn_wk_w, L0_attn_wv_w)]).T
    b_qkv = np.concatenate([np.asarray(w) for w in (L0_attn_wq_b, L0_attn_wk_b, L0_attn_wk_b, L0_attn_wk_b, L0_attn_wv_b)])
    arrays = {
        "x_t": np.ascontiguousarray(blocks),
        "x": flat,
        "w_qkv": by_partition(w_qkv),
        "b_qkv": np.ascontiguousarray(b_qkv.reshape(-1, P).T),
        "w_o": by_partition(np.asarray(L0_attn_wo_w).T),
        "b_o": np.ascontiguousarray(np.broadcast_to(np.asarray(L0_attn_wo_b), (P, D))),
        "w_f": by_partition(np.asarray(L0_ffn_weight)),
    }
    nc = bacc.Bacc("TRN2", target_bir_lowering=False, num_devices=1)
    aps = {n: nc.dram_tensor(n, a.shape, mybir.dt.from_np(a.dtype), kind="ExternalInput").ap() for n, a in arrays.items()}
    out = nc.dram_tensor("out", (B * T, D), F32, kind="ExternalOutput").ap()
    build(nc, out=out, B=B, T=T, H=HEADS, **aps)
    r = run_bass_kernel_spmd(nc, [arrays], core_ids=[0])
    return r.results[0]["out"].reshape(B, T, D)
```

```python
from contextlib import ExitStack

import concourse.bass as bass
from concourse import mybir

F32 = mybir.dt.float32
F32R = mybir.dt.float32r
BF16 = mybir.dt.bfloat16
I32 = mybir.dt.int32
ALU = mybir.AluOpType
ACT = mybir.ActivationFunctionType
AX = mybir.AxisListType
RMAX = bass.bass_isa.ReduceOp.max

P = 128
FP8_MAX = 448.0
SCALE_EPS = 1e-12
LN_EPS = 1e-5
EXP_SAFE = 60.0
MASKED = -3.0e38


def build(nc, x_t, x, w_qkv, b_qkv, w_o, b_o, w_f, out, B, T, H):
    D = x.shape[1]
    HD = D // H
    KT = D // P
    NB = 512
    TB = B * T // NB
    JB = T // NB
    QT = NB // P
    TT = T // P
    TILES = B * TT
    HG = P // HD
    G = H // HG
    MT = G + 1
    NH = D // 512
    SR = 3 * HD
    SM = SR + 2
    SCALE = float(HD) ** -0.5
    SAFE_NORMS = (EXP_SAFE / SCALE) ** 2
    SLOTS = QT
    LN = 7
    LN2 = 6
    assert HG == 4 and NH == 2 and TB == KT and G == 2 * QT and JB % 2 == 0 and TILES % 4 == 0

    q_hi_d = nc.dram_tensor("q_hi_d", (TB, H * HD, NB), F32).ap()
    q_lo_d = nc.dram_tensor("q_lo_d", (TB, H * HD, NB), F32).ap()
    k_st_d = nc.dram_tensor("k_st_d", (TB, SR, NB), F32).ap()
    v_d = nc.dram_tensor("v_d", (TB, P, QT, HD), F32).ap()
    max_d = nc.dram_tensor("max_d", (2, TB, H, NB), F32).ap()
    x1_d = nc.dram_tensor("x1_d", (TILES, P, D), F32).ap()
    x_tiles = x.rearrange("(n p) d -> n p d", p=P)
    out_tiles = out.rearrange("(n p) d -> n p d", p=P)

    ctx = ExitStack()

    def sem(name):
        return ctx.enter_context(nc.semaphore(name))

    with ctx:
        def sb(name, shape, dt=F32, stack=ctx):
            return stack.enter_context(nc.sbuf_tensor(name, shape, dt))

        ident = sb("ident", [P, P])
        ident_bf = sb("ident_bf", [P, P], BF16)
        mask_bf = sb("mask_bf", [P, P], BF16)
        amax_x = sb("amax_x", [P, TILES])
        amax_w = sb("amax_w", [P, KT])
        small = sb("small", [P, 32])
        exponent = sb("exponent", [P, 1])
        flag = sb("flag", [P, 1], I32)

        with ExitStack() as s:
            w_hi = sb("w_hi", [P, MT, KT, P], F32R, s)
            w_lo = sb("w_lo", [P, MT, KT, P], F32R, s)
            xt_raw = sb("xt_raw", [P, KT, NB], F32, s)
            xt_hi = sb("xt_hi", [P, 2, KT, NB], F32R, s)
            xt_lo0 = sb("xt_lo0", [P, KT, NB], F32R, s)
            with ExitStack() as s_stage:
                w_stage = sb("w_stage", [P, 2, KT, P], F32, s_stage)
            xt_lo1 = sb("xt_lo1", [P, KT, NB], F32R, s)
            kv = sb("kv", [P, TB, NB], F32, s)
            bias = sb("bias", [P, MT], F32, s)
            head_sum = sb("head_sum", [P, P], F32R, s)
            raw = sb("raw", [P, 2, NB], F32, s)
            sq = sb("sq", [P, 2, NB], F32R, s)
            part_hi = sb("part_hi", [P, 2, NB], F32R, s)
            part_lo = sb("part_lo", [P, 2, NB], F32R, s)
            wf_tile = sb("wf_tile", [P, D], F32, s)
            v_t = sb("v_t", [P, TB, QT, HD], F32, s)
            norms = sb("norms", [P, TB, MT], F32, s)
            centre = sb("centre", [P, B], F32, s)
            zeros = sb("zeros", [P, NB], F32, s)
            xt_lo = (xt_lo0, xt_lo1)
            k_hi = xt_hi[:, :, 0:JB]
            k_lo = [lo[:, 0:JB] for lo in xt_lo]

        with ExitStack() as s:
            wo_hi = sb("wo_hi", [P, KT, D], F32R, s)
            wo_lo = sb("wo_lo", [P, KT, D], F32R, s)
            with ExitStack() as s_stage:
                wo_stage = sb("wo_stage", [P, 2, D], F32, s_stage)
            with ExitStack() as s_maxima:
                q_m = sb("q_m", [SR, 2, T], F32R, s_maxima)
                k_m = sb("k_m", [SR, T], F32R, s_maxima)
                row_max = sb("row_max", [P, TT], F32, s_maxima)
                max_hi = sb("max_hi", [TT, P], F32R, s_maxima)
                max_lo = sb("max_lo", [TT, P], F32R, s_maxima)
            bo = sb("bo", [P, D], F32, s)
            res = sb("res", [P, D], F32, s)
            k_st = sb("k_st", [SM, T], F32R, s)
            v_sb = sb("v_sb", [P, TT, HD], F32, s)
            q_st = sb("q_st", [SM, 2, HG, NB], F32R, s)
            acc = sb("acc", [P, 2, HG, NB], F32, s)
            with ExitStack() as s_prob:
                prob = sb("prob", [P, SLOTS, HG, NB], F32, s_prob)
            with ExitStack() as s_end:
                end_res = sb("end_res", [P, 2, D], F32, s_end)
                end_hi = sb("end_hi", [P, 2, KT, P], F32R, s_end)
                end_lo = sb("end_lo", [P, 2, KT, P], F32R, s_end)
            s.enter_context(nc.sbuf_tensor("prob_place", [P, SLOTS, HG, NB], F32))
            ones = sb("ones", [P, HD], F32, s)
            r_den = sb("r_den", [P, NB], F32, s)
            att = sb("att", [P, 2 * G, NB], F32, s)
            att_hi = sb("att_hi", [P, KT, P], F32R, s)
            att_lo = sb("att_lo", [P, KT, P], F32R, s)
            stats = sb("stats", [P, 2, NH, 6], F32, s)
            moments = sb("moments", [P, 2, 4], F32, s)

        with ExitStack() as s:
            wf_hi = sb("wf_hi", [P, KT, D], F32R, s)
            wf_lo = sb("wf_lo", [P, KT, D], F32R, s)
            wf = sb("wf", [P, KT, D], F32, s)
            x1 = sb("x1", [P, 4, D], F32, s)
            x_sim = sb("x_sim", [P, 2, D], F32, s)
            xs_hi = sb("xs_hi", [P, 2, KT, P], F32R, s)
            xs_lo = sb("xs_lo", [P, 2, KT, P], F32R, s)
            y2 = sb("y2", [P, 2, D], F32, s)
            stats2 = sb("stats2", [P, 2, NH, 6], F32, s)
            moments2 = sb("moments2", [P, 2, 4], F32, s)

        bank = ctx.enter_context(nc.psum_tensor("bank", [P, 8, 512], F32))
        Y_BANK, DEN_BANK, KV_BANK = 7, 6, 6

        consts = sem("consts")
        passed = sem("passed")
        w_in = [sem("w_in0"), sem("w_in1")]
        w_hi_cut, w_cut = sem("w_hi_cut"), sem("w_cut")
        b_in = sem("b_in")
        zeros_sent = sem("zeros_sent")
        xt_in = sem("xt_in")
        xt_hi_cut, xt_cut = sem("xt_hi_cut"), sem("xt_cut")
        wf_tile_in = sem("wf_tile_in")
        wf_tile_read = sem("wf_tile_read")
        qkv_done = sem("qkv_done")
        raw_ready = sem("raw_ready")
        sq_ready = sem("sq_ready")
        norm_done = sem("norm_done")
        norm_read = sem("norm_read")
        hi_cut = sem("hi_cut")
        lo_cut = sem("lo_cut")
        part_sent = [sem("part_sent0"), sem("part_sent1")]
        k_steps = sem("k_steps")
        k_sq = sem("k_sq")
        k_norm_done = sem("k_norm_done")
        k_norm_read = sem("k_norm_read")
        v_turned = sem("v_turned")
        kv_sent = sem("kv_sent")
        bound_steps = sem("bound_steps")
        bound_all = sem("bound_all")
        flag_ready = sem("flag_ready")
        project_over = sem("project_over")

        m_k_in = sem("m_k_in")
        m_q_in = [sem("m_q_in0"), sem("m_q_in1")]
        m_s_done = sem("m_s_done")
        m_s_read = sem("m_s_read")
        m_turned = sem("m_turned")
        m_hi_cut, m_lo_cut = sem("m_hi_cut"), sem("m_lo_cut")
        m_sent = sem("m_sent")
        attend_go = sem("attend_go")

        wo_in = [sem("wo_in0"), sem("wo_in1")]
        wo_hi_cut, wo_cut = sem("wo_hi_cut"), sem("wo_cut")
        bo_in = sem("bo_in")
        fixed = sem("fixed")
        kv_in = sem("kv_in")
        q_in = sem("q_in")
        s_done = sem("s_done")
        p_done = sem("p_done")
        masked = sem("masked")
        pv_done = sem("pv_done")
        acc_done = sem("acc_done")
        den_done = sem("den_done")
        den_read = sem("den_read")
        att_ready = sem("att_ready")
        att_hi_cut = sem("att_hi_cut")
        att_cut = sem("att_cut")
        y_done = sem("y_done")
        y_read = sem("y_read")
        res_in = sem("res_in")
        end_in = [sem("end_in0"), sem("end_in1")]
        res_ready = sem("res_ready")
        ln1 = sem("ln1")
        x1_sent = sem("x1_sent")
        end_sent = [sem("end_sent0"), sem("end_sent1")]

        wf_in = [sem(f"wf_in{k}") for k in range(KT)]
        scale_steps = sem("scale_steps")
        wf_clip, wf_hi_cut, wf_cut = sem("wf_clip"), sem("wf_hi_cut"), sem("wf_cut")
        g_all = sem("g_all")
        x1_in = [sem(f"x1_in{i}") for i in range(4)]
        sim_ready = sem("sim_ready")
        t_done = sem("t_done")
        t_hi = sem("t_hi")
        t_lo = sem("t_lo")
        f_done = sem("f_done")
        f_read = sem("f_read")
        ln2 = sem("ln2")
        y_sent = [sem("y_sent0"), sem("y_sent1")]

        SEQ_STEPS = G * QT * JB * (JB + 1) // 2
        SEQ_GROUPS = JB * G

        def key_tiles(j):
            return QT * (j + 1)

        def group(b, j, gp, r):
            return b * SEQ_GROUPS + (j * G + r) + gp * 2

        def step(b, j, gp, r):
            n = key_tiles(j)
            return b * SEQ_STEPS + (G * QT * j * (j + 1) // 2 + r * n) + gp * (2 * n)

        def projected(b, j, gp):
            return b * TT + (j - 1) * QT + gp

        def stored_alone(b, j, gp):
            return b * (TT - QT) + (j - 1) * QT + gp

        def first_query(j, t):
            return P * max(0, t - QT * j)

        def pairs_of_groups(eng, b, body):
            for j in range(JB):
                first, last = int(j == 0), int(j == JB - 1)
                if first:
                    body(j, 0, True, False)
                with eng.Fori(first, G // 2 - last) as gp:
                    body(j, gp, False, False)
                if last:
                    body(j, G // 2 - 1, False, True)

        def projection_steps(j, r):
            half = key_tiles(j) // 2
            return range(half + 1, key_tiles(j)) if r == 0 else range(3, half + 3)

        def wait_apart(eng, semaphore, value):
            eng.wait_ge(semaphore, value)
            eng.sem_inc(passed, 1)

        def one(ap):
            return ap.rearrange("p a n -> p (a n)")

        def flat(ap):
            return ap.rearrange("p k n -> p (k n)")

        block = ctx.enter_context(nc.Block())

        @block.sync
        def _(sp):
            sp.dma_start(bias[:], b_qkv).then_inc(b_in, 16)

            def load_w(m):
                if m >= 2:
                    sp.wait_ge(w_cut, m - 1)
                sp.dma_start(w_stage[:, m % 2], w_qkv[:, m]).then_inc(w_in[m % 2], 16)

            load_w(0)
            for half in range(2):
                k = slice(half * KT // 2, (half + 1) * KT // 2)
                sp.dma_start(xt_raw[:, k], x_t[0, :, k]).then_inc(xt_in, 16)
                sp.wait_ge(xt_in, 16 * (half + 1))
            for m in range(1, MT):
                load_w(m)
            sp.dma_start(wf_tile[:], w_f[:, 0]).then_inc(wf_tile_in, 16)
            with sp.Fori(1, TB) as tb:
                for half in range(2):
                    k = slice(half * KT // 2, (half + 1) * KT // 2)
                    sp.wait_ge(xt_cut, tb * 2 + (half + 1))
                    sp.dma_start(xt_raw[:, k], x_t[bass.ds(tb, 1), :, k].rearrange("a p k n -> p (a k) n")).then_inc(xt_in, 16)
                    wait_apart(sp, xt_in, tb * 32 + 16 * (half + 1))
                sp.wait_ge(wf_tile_read, tb + 1)
                sp.dma_start(wf_tile[:], one(w_f[:, bass.ds(tb, 1)])).then_inc(wf_tile_in, 16)

            sp.wait_ge(qkv_done, (TB + 2) * MT)
            for k in range(KT):
                if k >= 2:
                    sp.wait_ge(wo_cut, k - 1)
                sp.dma_start(wo_stage[:, k % 2], w_o[:, k]).then_inc(wo_in[k % 2], 16)
            for s in part_sent:
                sp.wait_ge(s, 32 * (TB * G // 2 + 1))
            sp.wait_ge(kv_sent, 16 * (2 * B + TB))
            sp.wait_ge(zeros_sent, 32 * H * TB // P)
            sp.wait_ge(flag_ready, 1)
            sp.wait_ge(wo_cut, KT)
            sp.sem_inc(project_over, 1)

            needed = sp.value_load(flag[0:1, 0:1], min_val=0, max_val=1)
            with sp.If(needed == 1):
                q_hi_m = q_hi_d.rearrange("t (h p) n -> h p t n", p=HD)
                q_lo_m = q_lo_d.rearrange("t (h p) n -> h p t n", p=HD)
                with sp.Fori(0, B) as b:
                    blocks = bass.ds(b * JB, JB)
                    sp.wait_ge(m_turned, b * H + 2)
                    sp.dma_start(k_m[:].bitcast(F32).rearrange("r (t n) -> r t n", n=NB), k_st_d[blocks].rearrange("t r n -> r t n")).then_inc(m_k_in, 16)
                    with sp.Fori(0, H // 2) as hp:
                        for r in range(2):
                            n = b * H + r + hp * 2
                            head = bass.ds(hp * 2 + r, 1)
                            sp.wait_ge(m_turned, n + 1)
                            for rows, src in ((0, q_hi_m), (HD, q_lo_m), (2 * HD, q_hi_m)):
                                sp.dma_start(q_m[rows:rows + HD, r].bitcast(F32).rearrange("p (t n) -> p t n", n=NB),
                                             src[head, :, blocks].rearrange("a p t n -> (a p) t n")).then_inc(m_q_in[r], 16)
                sp.wait_ge(m_sent, 32 * JB * (B * H + 1))
            sp.sem_inc(attend_go, 1)

            sp.dma_start(bo[:], b_o).then_inc(bo_in, 16)
            q_hi_h = q_hi_d.rearrange("t (h p) n -> (t h) p n", p=HD)
            q_lo_h = q_lo_d.rearrange("t (h p) n -> (t h) p n", p=HD)
            max_h = max_d.rearrange("c t h n -> c (t h) n")

            def load_q(n, slot):
                heads = bass.ds(n * HG, HG)
                sp.dma_start(q_st[0:HD, slot].bitcast(F32), q_hi_h[heads].rearrange("h p n -> p h n")).then_inc(q_in, 16)
                sp.dma_start(q_st[HD:2 * HD, slot].bitcast(F32), q_lo_h[heads].rearrange("h p n -> p h n")).then_inc(q_in, 16)
                sp.dma_start(q_st[2 * HD:SR, slot].bitcast(F32), q_hi_h[heads].rearrange("h p n -> p h n")).then_inc(q_in, 16)
                sp.dma_start(q_st[SR:SM, slot].bitcast(F32), max_h[:, heads]).then_inc(q_in, 16)
                wait_apart(sp, q_in, n * 64 + 64)

            with sp.Fori(0, B) as b:
                sp.wait_ge(den_done, b * SEQ_GROUPS + 2)
                blocks = bass.ds(b * JB, JB)
                sp.dma_start(k_st[0:SR].bitcast(F32).rearrange("r (t n) -> r t n", n=NB), k_st_d[blocks].rearrange("t r n -> r t n")).then_inc(kv_in, 16)
                sp.dma_start(v_sb[:].rearrange("p (t q) d -> p t (q d)", q=QT), v_d[blocks].rearrange("t p q d -> p t (q d)")).then_inc(kv_in, 16)
                load_q(b * SEQ_GROUPS, 0)

                def body(j, gp, first, last):
                    if j > 0:
                        tile = projected(b, j, gp)
                        sp.wait_ge(x1_sent, stored_alone(b, j, gp) * 16 + 16)
                        sp.wait_ge(ln1, tile * LN + LN)
                        sp.dma_start(res[:], x_tiles[bass.ds(tile, 1)].rearrange("a p d -> p (a d)")).then_inc(res_in, 16)
                    for r in range(2):
                        if not (last and r == 1):
                            sp.wait_ge(s_done, step(b, j, gp, r) * 2 + 1)
                            load_q(group(b, j, gp, r) + 1, 1 - r)
                    if j > 0:
                        sp.wait_ge(ln1, tile * LN + (LN + 6))
                        sp.dma_start(x1_d[bass.ds(tile, 1)].rearrange("a p d -> p (a d)"), res[:]).then_inc(x1_sent, 16)

                pairs_of_groups(sp, b, body)
                for t in range(QT):
                    tile = projected(b, JB, t)
                    if t >= 2:
                        sp.wait_ge(end_sent[t % 2], b * 32 + 48)
                        sp.wait_ge(ln1, tile * LN)
                    else:
                        sp.wait_ge(pv_done, (b + 1) * SEQ_STEPS + SLOTS)
                        sp.wait_ge(acc_done, (b + 1) * SEQ_STEPS + SLOTS)
                    sp.dma_start(end_res[:, t % 2], x_tiles[bass.ds(tile, 1)].rearrange("a p d -> p (a d)")).then_inc(end_in[t % 2], 16)

            for s in end_sent:
                sp.wait_ge(s, 32 * B + 32)
            sp.wait_ge(x1_sent, 16 * (TILES - B * QT + 1))
            sp.wait_ge(ln1, LN * (TILES + 1))
            for k in range(KT):
                sp.dma_start(wf[:, k], w_f[:, k]).then_inc(wf_in[k], 16)
            with sp.Fori(0, TILES // 4) as i:
                for r in range(4):
                    sp.wait_ge(f_read, i * 4 + r + 1)
                    sp.dma_start(x1[:, r], x1_d[bass.ds(i * 4 + r, 1)].rearrange("a p d -> p (a d)")).then_inc(x1_in[r], 16)
            for i in range(2):
                sp.wait_ge(y_sent[i], 16 * (TILES // 2 + 1))

        @block.gpsimd
        def _(pool):
            pool.sem_inc(xt_cut, 2)
            nc.gpsimd.memset(ident[:], 0.0).then_inc(consts, 1)
            nc.gpsimd.memset(mask_bf[:], 0.0).then_inc(consts, 1)
            nc.gpsimd.memset(head_sum[:].bitcast(F32), 0.0).then_inc(consts, 1)
            nc.gpsimd.memset(zeros[:], 0.0).then_inc(consts, 1)
            nc.gpsimd.memset(exponent[:], -0.5).then_inc(consts, 1)
            pool.wait_ge(consts, 5)
            nc.gpsimd.affine_select(out=ident[:], in_=ident[:], compare_op=ALU.not_equal, fill=1.0,
                                    base=0, pattern=[[-1, P]], channel_multiplier=1).then_inc(consts, 1)
            nc.gpsimd.affine_select(out=mask_bf[:], in_=mask_bf[:], compare_op=ALU.is_ge, fill=MASKED,
                                    base=0, pattern=[[-1, P]], channel_multiplier=1).then_inc(consts, 1)
            for h in range(HG):
                pool.wait_ge(consts, 7 + h)
                nc.gpsimd.memset(head_sum[h * HD:(h + 1) * HD, h * HD:(h + 1) * HD].bitcast(F32), 1.0).then_inc(consts, 1)
            pool.wait_ge(consts, 7 + HG)
            nc.gpsimd.tensor_copy(ident_bf[:], ident[:]).then_inc(consts, 1)

            def inverse_deviation(moments, done, before):
                wait_apart(pool, done, before + (NH + 1))
                nc.gpsimd.tensor_scalar(moments[:, 1:2], moments[:, 1:2], LN_EPS, None, ALU.add).then_inc(done, 1)
                wait_apart(pool, done, before + (NH + 2))
                nc.gpsimd.tensor_tensor(moments[:, 2:3], moments[:, 1:2], exponent[:], ALU.pow).then_inc(done, 1)

            with pool.Fori(0, TB // 2) as i:
                for r in range(2):
                    tb = i * 2 + r
                    wait_apart(pool, qkv_done, tb * MT + MT)
                    if r == 1:
                        pool.wait_ge(w_cut, MT)
                    for half in range(2):
                        k = slice(half * KT // 2, (half + 1) * KT // 2)
                        u = tb * 2 + half
                        wait_apart(pool, xt_in, u * 16 + 16)
                        nc.gpsimd.tensor_copy(xt_hi[:, r, k], xt_raw[:, k]).then_inc(xt_hi_cut, 1)
                        pool.wait_ge(xt_hi_cut, u + 1)
                        nc.gpsimd.tensor_tensor(xt_lo[r][:, k], xt_raw[:, k], xt_hi[:, r, k].bitcast(F32), ALU.subtract).then_inc(xt_cut, 1)
            for k in range(KT):
                pool.wait_ge(wo_hi_cut, k + 1)
                nc.gpsimd.tensor_tensor(wo_lo[:, k], wo_stage[:, k % 2], wo_hi[:, k].bitcast(F32), ALU.subtract).then_inc(wo_cut, 1)
            pool.wait_ge(bound_steps, 4)
            nc.gpsimd.partition_all_reduce(small[:, 3:6], small[:, 0:3], P, RMAX).then_inc(bound_all, 1)

            pool.wait_ge(attend_go, 1)
            nc.gpsimd.memset(k_st[SR:SM].bitcast(F32), -1.0).then_inc(fixed, 1)
            pool.wait_ge(fixed, 1)
            nc.gpsimd.memset(ones[:], 1.0).then_inc(fixed, 1)
            pool.wait_ge(fixed, 2)
            pool.wait_ge(bo_in, 16)
            with pool.Fori(0, B) as b:
                def body(j, gp, first, last):
                    if j > 0:
                        tile = projected(b, j, gp)
                        pool.wait_ge(res_in, stored_alone(b, j, gp) * 16 + 16)
                        nc.gpsimd.tensor_tensor(res[:], res[:], bo[:], ALU.add).then_inc(res_ready, 1)
                        wait_apart(pool, att_hi_cut, tile + 1)
                        heads = att[:, (j - 1) % 2 * G:(j - 1) % 2 * G + G, bass.ds(gp * P, P)]
                        nc.gpsimd.tensor_tensor(att_lo[:], heads, att_hi[:].bitcast(F32), ALU.subtract).then_inc(att_cut, 1)
                    for r in range(2):
                        n, s0 = group(b, j, gp, r), step(b, j, gp, r)
                        for i in range(QT):
                            t = QT * j + i
                            off = first_query(j, t)
                            wait_apart(pool, p_done, s0 * 2 + (2 * t + 4))
                            tri = prob[:, t % SLOTS, :, off:off + P]
                            nc.gpsimd.affine_select(out=tri, in_=tri, compare_op=ALU.is_ge, fill=0.0, base=0,
                                                    pattern=[[0, HG], [1, P]], channel_multiplier=-1).then_inc(masked, 1)
                    if j > 0:
                        inverse_deviation(moments[:, 0], ln1, tile * LN + LN)

                pairs_of_groups(pool, b, body)
                for t in range(QT):
                    tile = projected(b, JB, t)
                    pool.wait_ge(end_in[t % 2], b * 32 + 16 * (t // 2 + 1))
                    nc.gpsimd.tensor_tensor(end_res[:, t % 2], end_res[:, t % 2], bo[:], ALU.add).then_inc(res_ready, 1)
                    pool.wait_ge(att_hi_cut, tile + 1)
                    heads = att[:, (JB - 1) % 2 * G:(JB - 1) % 2 * G + G, t * P:(t + 1) * P]
                    nc.gpsimd.tensor_tensor(end_lo[:, t % 2], heads, end_hi[:, t % 2].bitcast(F32), ALU.subtract).then_inc(att_cut, 1)
                    if t >= 1:
                        inverse_deviation(moments[:, (t - 1) % 2], ln1, (tile - 1) * LN + LN)
                inverse_deviation(moments[:, (QT - 1) % 2], ln1, projected(b, JB, QT - 1) * LN + LN)

            pool.wait_ge(scale_steps, 1)
            nc.gpsimd.partition_all_reduce(small[:, 9:10], small[:, 8:9], P, RMAX).then_inc(g_all, 1)
            pool.wait_ge(scale_steps, 5)

            def clip(i, r):
                n = i * 4 + r
                pool.wait_ge(x1_in[r % 4], i * 16 + 16 * (r // 4 + 1))
                wait_apart(pool, t_done, n + 1)
                nc.gpsimd.tensor_scalar(x_sim[:, r % 2], x1[:, r % 4], small[:, 14:15], FP8_MAX, ALU.mult, ALU.min).then_inc(sim_ready, 1)
                wait_apart(pool, sim_ready, n * 2 + 1)
                nc.gpsimd.tensor_scalar(x_sim[:, r % 2], x_sim[:, r % 2], -FP8_MAX, None, ALU.max).then_inc(sim_ready, 1)

            clip(0, 0)
            clip(0, 1)
            with pool.Fori(0, TILES // 4 - 1) as i:
                for r in range(4):
                    clip(i, r + 2)
                    inverse_deviation(moments2[:, r % 2], ln2, (i * 4 + r) * LN2)
            i = TILES // 4 - 1
            for r in range(4):
                if r < 2:
                    clip(i, r + 2)
                inverse_deviation(moments2[:, r % 2], ln2, (i * 4 + r) * LN2)

        @block.scalar
        def _(act):
            act.sem_inc(raw_ready, 2)
            act.sem_inc(sq_ready, 2)
            act.sem_inc(p_done, 2)
            for s in (*part_sent, *end_sent):
                act.sem_inc(s, 32)
            for s in (x1_sent, *y_sent):
                act.sem_inc(s, 16)
            act.wait_ge(consts, 5)
            for c in range(2):
                for i in range(TB * H // P):
                    act.dma_start(max_d[c].rearrange("t h n -> (t h) n")[i * P:(i + 1) * P], zeros[:]).then_inc(zeros_sent, 16)
            act.wait_ge(b_in, 16)

            def send(tb, m):
                act.wait_ge(lo_cut, tb * G + (m + 3))
                rows = slice(m * P, (m + 1) * P)
                act.dma_start(q_hi_d[bass.ds(tb, 1), rows].rearrange("a p n -> p (a n)"), part_hi[:, m % 2].bitcast(F32)).then_inc(part_sent[m % 2], 16)
                act.dma_start(q_lo_d[bass.ds(tb, 1), rows].rearrange("a p n -> p (a n)"), part_lo[:, m % 2].bitcast(F32)).then_inc(part_sent[m % 2], 16)

            with act.Fori(0, TB) as tb:
                for m in range(MT):
                    act.wait_ge(qkv_done, tb * MT + (m + 1 + 2 * MT))
                    if m == G:
                        nc.scalar.activation(one(kv[:, bass.ds(tb, 1)]), bank[:, KV_BANK], ACT.Identity, bias=bias[:, m:m + 1]).then_inc(raw_ready, 1)
                    else:
                        u = tb * G + m
                        act.wait_ge(lo_cut, u + 1)
                        nc.scalar.activation(raw[:, m % 2], bank[:, m % 2], ACT.Identity, bias=bias[:, m:m + 1]).then_inc(raw_ready, 1)
                        act.wait_ge(norm_done, u + 1)
                        nc.scalar.activation(sq[:, m % 2], bank[:, m % 2], ACT.Square, bias=bias[:, m:m + 1]).then_inc(sq_ready, 1)
                    if m >= 1:
                        send(tb, m - 1)
            for tb in range(TB):
                b = tb // JB
                act.wait_ge(k_steps, 5 * b + 3)
                act.wait_ge(norm_done, TB * G + 2)
                if tb >= 2:
                    act.wait_ge(k_norm_done, tb - 1)
                nc.scalar.activation(sq[0:HD, tb % 2], kv[0:HD, tb], ACT.Square).then_inc(k_sq, 1)
            act.wait_ge(k_steps, 5 * B + 1)
            act.dma_start(v_d.rearrange("t p q d -> p t (q d)"), v_t[:].rearrange("p t q d -> p t (q d)")).then_inc(kv_sent, 16 * TB)
            for b in range(B):
                act.wait_ge(k_steps, 5 * (b + 1))
                blocks = slice(b * JB, (b + 1) * JB)
                act.dma_start(k_st_d[blocks, 0:2 * HD].rearrange("t r n -> r t n"), k_hi[0:2 * HD, b].bitcast(F32)).then_inc(kv_sent, 16)
                act.dma_start(k_st_d[blocks, 2 * HD:SR].rearrange("t r n -> r t n"), k_lo[b][2 * HD:SR].bitcast(F32)).then_inc(kv_sent, 16)
            for k in range(KT):
                act.wait_ge(wo_in[k % 2], 16 * (k // 2 + 1))
                nc.scalar.activation(wo_hi[:, k], wo_stage[:, k % 2], ACT.Copy).then_inc(wo_hi_cut, 1)

            act.wait_ge(flag_ready, 1)
            needed = act.value_load(flag[0:1, 0:1], min_val=0, max_val=1)
            with act.If(needed == 1):
                act.sem_inc(m_sent, 32 * JB)
                with act.Fori(0, B) as b:
                    with act.Fori(0, H) as h:
                        act.wait_ge(m_lo_cut, b * H + h + 2)
                        for c, part in ((0, max_hi), (1, max_lo)):
                            for j in range(JB):
                                act.dma_start(max_d[c].rearrange("t h (q p) -> (t h) q p", p=P)[bass.ds(b * (JB * H) + j * H + h, 1)].rearrange("a q p -> (a q) p"),
                                              part[j * QT:(j + 1) * QT].bitcast(F32)).then_inc(m_sent, 16)

            with act.Fori(0, B) as b:
                for e in end_sent:
                    act.wait_ge(e, b * 32 + 32)
                act.wait_ge(ln1, b * (TT * LN) + LN)

                def body(j, gp, first, last):
                    for r in range(2):
                        s0 = step(b, j, gp, r)
                        for t in range(key_tiles(j)):
                            off = first_query(j, t)
                            act.wait_ge(pv_done, s0 + (t + 1))
                            act.wait_ge(acc_done, s0 + (t + 1))
                            for p in range(2):
                                act.wait_ge(s_done, s0 * 2 + (2 * t + p + 2))
                                nc.scalar.activation(prob[:, t % SLOTS, 2 * p:2 * p + 2, off:NB], bank[:, 2 * p:2 * p + 2, off:NB],
                                                     ACT.Exp, scale=SCALE).then_inc(p_done, 1)
                            if j > 0 and r == 0 and t == key_tiles(j) // 2 - 1:
                                act.wait_ge(att_ready, b * SEQ_GROUPS + (j * G + 2))
                                act.wait_ge(y_done, projected(b, j, gp) * 2 + 4)
                                heads = att[:, (j - 1) % 2 * G:(j - 1) % 2 * G + G, bass.ds(gp * P, P)]
                                nc.scalar.activation(att_hi[:], heads, ACT.Copy).then_inc(att_hi_cut, 1)

                pairs_of_groups(act, b, body)

                def end_store(t):
                    tile = projected(b, JB, t)
                    act.wait_ge(ln1, tile * LN + (LN + 6))
                    act.dma_start(x1_d[bass.ds(tile, 1)].rearrange("a p d -> p (a d)"), end_res[:, t % 2]).then_inc(end_sent[t % 2], 16)

                for t in range(QT):
                    act.wait_ge(att_ready, b * SEQ_GROUPS + (SEQ_GROUPS + 2))
                    act.wait_ge(y_done, projected(b, JB, t) * 2 + 2)
                    heads = att[:, (JB - 1) % 2 * G:(JB - 1) % 2 * G + G, t * P:(t + 1) * P]
                    nc.scalar.activation(end_hi[:, t % 2], heads, ACT.Copy).then_inc(att_hi_cut, 1)
                    if t >= 2:
                        end_store(t - 2)
                end_store(QT - 2)
                end_store(QT - 1)

            for k in range(KT):
                act.wait_ge(wf_clip, 2 * k + 2)
                nc.scalar.activation(wf_hi[:, k], wf[:, k], ACT.Copy).then_inc(wf_hi_cut, 1)

            def upper(r, n):
                act.wait_ge(t_done, n + 3)
                act.wait_ge(f_done, n + 1)
                nc.scalar.activation(xs_hi[:, r % 2].rearrange("p k n -> p (k n)"),
                                     bank[:, 2 * (r % 2):2 * (r % 2) + 2].rearrange("p k n -> p (k n)"), ACT.Copy).then_inc(t_hi, 1)

            def store(r, n):
                act.wait_ge(ln2, n * LN2 + 6)
                act.dma_start(out_tiles[bass.ds(n, 1)].rearrange("a p d -> p (a d)"), y2[:, r % 2]).then_inc(y_sent[r % 2], 16)

            upper(0, 0)
            with act.Fori(0, TILES // 4 - 1) as i:
                for r in range(4):
                    upper(r + 1, i * 4 + r + 1)
                    store(r, i * 4 + r)
            i = TILES // 4 - 1
            for r in range(4):
                if r < 3:
                    upper(r + 1, i * 4 + r + 1)
                store(r, i * 4 + r)

        @block.vector
        def _(dve):
            def moments_of(z, stats, moments, done, before):
                for h in range(NH):
                    nc.vector.bn_stats(stats[:, h], z[:, h * 512:(h + 1) * 512]).then_inc(done, 1)
                wait_apart(dve, done, before + NH)
                nc.vector.bn_aggr(moments[:, 0:2], stats[:]).then_inc(done, 1)

            def normalise(z, moments, done, before):
                dve.wait_ge(done, before + (NH + 3))
                nc.vector.tensor_scalar(z, z, moments[:, 0:1], moments[:, 2:3], ALU.subtract, ALU.mult).then_inc(done, 1)

            dve.sem_inc(wf_tile_read, 1)
            dve.sem_inc(norm_read, 2)
            dve.sem_inc(lo_cut, 2)
            dve.sem_inc(acc_done, SLOTS)
            dve.sem_inc(den_read, 1)
            dve.sem_inc(att_ready, 2)
            dve.sem_inc(y_read, 2)
            dve.sem_inc(ln1, LN)
            dve.sem_inc(t_lo, 2)
            dve.sem_inc(f_read, 4)
            for m in range(MT):
                dve.wait_ge(w_in[m % 2], 16 * (m // 2 + 1))
                nc.vector.tensor_copy(w_hi[:, m], w_stage[:, m % 2]).then_inc(w_hi_cut, 1)
                dve.wait_ge(w_hi_cut, m + 1)
                nc.vector.tensor_tensor(w_lo[:, m], w_stage[:, m % 2], w_hi[:, m].bitcast(F32), ALU.subtract).then_inc(w_cut, 1)

            def norm(tb, m):
                dve.wait_ge(norm_done, tb * G + (m + 3))
                nc.vector.reduce_max(norms[:, bass.ds(tb, 1), m:m + 1].rearrange("p a b -> p (a b)"), bank[:, 2 + m % 2], AX.X).then_inc(norm_read, 1)

            with dve.Fori(0, TB) as tb:
                for m in range(G):
                    u = tb * G + m
                    dve.wait_ge(raw_ready, tb * MT + (m + 3))
                    dve.wait_ge(part_sent[m % 2], tb * (16 * G) + 32 * (m // 2 + 1))
                    nc.vector.tensor_copy(part_hi[:, m % 2], raw[:, m % 2]).then_inc(hi_cut, 1)
                    dve.wait_ge(hi_cut, u + 1)
                    nc.vector.tensor_tensor(part_lo[:, m % 2], raw[:, m % 2], part_hi[:, m % 2].bitcast(F32), ALU.subtract).then_inc(lo_cut, 1)
                    if m >= 1:
                        norm(tb, m - 1)
                    if m == 1:
                        dve.wait_ge(wf_tile_in, tb * 16 + 16)
                        nc.vector.tensor_reduce(amax_w[:, bass.ds(tb, 1)], wf_tile[:], AX.X, ALU.max, apply_absolute_value=True).then_inc(wf_tile_read, 1)
                norm(tb, G - 1)

            dve.wait_ge(raw_ready, TB * MT + 2)
            for b in range(B):
                keys = kv[0:SR, b * JB:(b + 1) * JB]
                nc.vector.tensor_reduce(centre[0:SR, b:b + 1], keys, AX.XY, ALU.add).then_inc(k_steps, 1)
                dve.wait_ge(k_steps, 5 * b + 1)
                nc.vector.tensor_scalar(centre[0:SR, b:b + 1], centre[0:SR, b:b + 1], 1.0 / T, None, ALU.mult).then_inc(k_steps, 1)
                dve.wait_ge(k_steps, 5 * b + 2)
                nc.vector.tensor_scalar(keys, keys, centre[0:SR, b:b + 1], None, ALU.subtract).then_inc(k_steps, 1)
                dve.wait_ge(k_steps, 5 * b + 3)
                nc.vector.tensor_copy(k_hi[0:SR, b], keys).then_inc(k_steps, 1)
                dve.wait_ge(k_steps, 5 * b + 4)
                nc.vector.tensor_tensor(k_lo[b][0:SR], keys, k_hi[0:SR, b].bitcast(F32), ALU.subtract).then_inc(k_steps, 1)
            dve.wait_ge(v_turned, 1)
            nc.vector.tensor_copy(v_t[:].rearrange("p t q d -> p (t q d)"), bank[:, 0:2].rearrange("p a n -> p (a n)")).then_inc(k_steps, 1)
            for tb in range(TB):
                dve.wait_ge(k_norm_done, tb + 1)
                nc.vector.reduce_max(norms[:, tb, G:MT], bank[:, 2 + tb % 2], AX.X).then_inc(k_norm_read, 1)

            dve.wait_ge(norm_read, TB * G + 2)
            dve.wait_ge(k_norm_read, TB)
            dve.wait_ge(wf_tile_read, KT + 1)
            nc.vector.memset(small[:, 0:3], 0.0).then_inc(bound_steps, 1)
            dve.wait_ge(bound_steps, 1)
            nc.vector.tensor_reduce(small[:, 0:1], norms[:, :, 0:G], AX.XY, ALU.max).then_inc(bound_steps, 1)
            nc.vector.tensor_reduce(small[0:HD, 1:2], one(norms[0:HD, :, G:MT]), AX.X, ALU.max).then_inc(bound_steps, 1)
            nc.vector.tensor_reduce(small[:, 2:3], amax_w[:], AX.X, ALU.max).then_inc(bound_steps, 1)
            dve.wait_ge(bound_all, 1)
            nc.vector.tensor_tensor(small[:, 6:7], small[:, 3:4], small[:, 4:5], ALU.mult).then_inc(bound_steps, 1)
            dve.wait_ge(bound_steps, 5)
            nc.vector.tensor_scalar(flag[:], small[:, 6:7], SAFE_NORMS, None, ALU.is_gt).then_inc(flag_ready, 1)

            dve.wait_ge(flag_ready, 1)
            needed = dve.value_load(flag[0:1, 0:1], min_val=0, max_val=1)
            with dve.If(needed == 1):
                dve.sem_inc(m_s_read, 2)
                dve.sem_inc(m_lo_cut, 1)
                dve.wait_ge(project_over, 1)
                with dve.Fori(0, B) as b:
                    with dve.Fori(0, H) as h:
                        n = b * H + h
                        for q in range(TT):
                            scores = bank[:, 4 * (q % 2):4 * (q % 2) + 4].rearrange("p a n -> p (a n)")[:, 0:(q + 1) * P]
                            dve.wait_ge(m_s_done, n * TT + (q + 1))
                            nc.vector.reduce_max(row_max[:, q:q + 1], scores, AX.X).then_inc(m_s_read, 1)
                        dve.wait_ge(m_turned, n + 3)
                        dve.wait_ge(m_sent, n * (32 * JB) + 32 * JB)
                        nc.vector.tensor_copy(max_hi[:], bank[0:TT, 0, 0:P]).then_inc(m_hi_cut, 1)
                        dve.wait_ge(m_hi_cut, n + 1)
                        nc.vector.tensor_tensor(max_lo[:], bank[0:TT, 0, 0:P], max_hi[:].bitcast(F32), ALU.subtract).then_inc(m_lo_cut, 1)

            def normalise_group(n, r, slot):
                dve.wait_ge(den_done, n + 3)
                nc.vector.reciprocal(r_den[:], bank[:, DEN_BANK]).then_inc(den_read, 1)
                dve.wait_ge(den_read, n + 2)
                nc.vector.tensor_tensor(slot, bank[:, 4 + r], r_den[:], ALU.mult).then_inc(att_ready, 1)

            def add_residual(z, tile, half, y_bank):
                cols = slice(half * 512, (half + 1) * 512)
                dve.wait_ge(y_done, tile * 2 + (half + 5))
                dve.wait_ge(res_ready, tile + 1)
                nc.vector.tensor_tensor(z[:, cols], bank[:, y_bank], z[:, cols], ALU.add).then_inc(y_read, 1)

            def largest(z, tile):
                dve.wait_ge(ln1, tile * LN + (LN + 6))
                nc.vector.tensor_reduce(amax_x[:, bass.ds(tile, 1)], z, AX.X, ALU.max, apply_absolute_value=True).then_inc(ln1, 1)

            with dve.Fori(0, B) as b:
                def body(j, gp, first, last):
                    for r in range(2):
                        n, s0 = group(b, j, gp, r), step(b, j, gp, r)
                        NT = key_tiles(j)
                        dve.wait_ge(den_done, n + 1)
                        for t in range(NT):
                            off = first_query(j, t)
                            if t >= 1:
                                dve.wait_ge(p_done, s0 * 2 + (2 * t + 4))
                                if t >= QT * j:
                                    dve.wait_ge(masked, n * QT + (t - QT * j + 1))
                                new = prob[:, t % SLOTS, :, off:NB]
                                if t == 1:
                                    if off > 0:
                                        nc.vector.tensor_copy(acc[:, r, :, 0:off], prob[:, 0, :, 0:off])
                                    nc.vector.tensor_tensor(acc[:, r, :, off:NB], prob[:, 0, :, off:NB], new, ALU.add).then_inc(acc_done, 2)
                                else:
                                    dve.wait_ge(acc_done, s0 + (t + SLOTS))
                                    nc.vector.tensor_tensor(acc[:, r, :, off:NB], acc[:, r, :, off:NB], new, ALU.add).then_inc(acc_done, 1)
                            if t == 2 and not (first and r == 0):
                                at = (gp * 2 + (j % 2 * G + r + 2 * G - 1)) % (2 * G)
                                normalise_group(n - 1, 1 - r, one(att[:, bass.ds(at, 1)]))
                            if j > 0:
                                tile = projected(b, j, gp)
                                if r == 1 and t == 1:
                                    add_residual(res[:], tile, 0, Y_BANK)
                                if r == 1 and t == min(NT // 2 + 3, NT - 1):
                                    add_residual(res[:], tile, 1, Y_BANK)
                                    dve.wait_ge(y_read, tile * 2 + 4)
                                    moments_of(res[:], stats[:, 0], moments[:, 0], ln1, tile * LN + LN)
                                if r == 1 and t == NT - 1:
                                    normalise(res[:], moments[:, 0], ln1, tile * LN + LN)
                                    largest(res[:], tile)

                pairs_of_groups(dve, b, body)
                normalise_group(b * SEQ_GROUPS + (SEQ_GROUPS - 1), 1, att[:, (JB - 1) % 2 * G + G - 1])

                def end_normalise(t):
                    tile = projected(b, JB, t)
                    normalise(end_res[:, t % 2], moments[:, t % 2], ln1, tile * LN + LN)
                    largest(end_res[:, t % 2], tile)

                for t in range(QT):
                    tile = projected(b, JB, t)
                    for half in range(2):
                        add_residual(end_res[:, t % 2], tile, half, Y_BANK - half)
                    dve.wait_ge(y_read, tile * 2 + 4)
                    if t >= 1:
                        end_normalise(t - 1)
                    moments_of(end_res[:, t % 2], stats[:, t % 2], moments[:, t % 2], ln1, tile * LN + LN)
                end_normalise(QT - 1)

            dve.wait_ge(ln1, LN * (TILES + 1))
            nc.vector.tensor_reduce(small[:, 8:9], amax_x[:], AX.X, ALU.max).then_inc(scale_steps, 1)
            nc.vector.tensor_copy(small[:, 10:11], small[:, 5:6]).then_inc(scale_steps, 1)
            dve.wait_ge(g_all, 1)
            dve.wait_ge(scale_steps, 2)
            nc.vector.tensor_scalar(small[:, 12:14], small[:, 9:11], SCALE_EPS, None, ALU.max).then_inc(scale_steps, 1)
            dve.wait_ge(scale_steps, 3)
            nc.vector.reciprocal(small[:, 16:18], small[:, 12:14]).then_inc(scale_steps, 1)
            dve.wait_ge(scale_steps, 4)
            nc.vector.tensor_scalar(small[:, 14:16], small[:, 16:18], FP8_MAX, None, ALU.mult).then_inc(scale_steps, 1)
            dve.wait_ge(scale_steps, 5)
            nc.vector.tensor_tensor(small[:, 18:19], small[:, 14:15], small[:, 15:16], ALU.mult).then_inc(scale_steps, 1)
            dve.wait_ge(scale_steps, 6)
            nc.vector.reciprocal(small[:, 19:20], small[:, 18:19]).then_inc(scale_steps, 1)
            for k in range(KT):
                dve.wait_ge(wf_in[k], 16)
                nc.vector.tensor_scalar(wf[:, k], wf[:, k], small[:, 15:16], FP8_MAX, ALU.mult, ALU.min).then_inc(wf_clip, 1)
                dve.wait_ge(wf_clip, 2 * k + 1)
                nc.vector.tensor_scalar(wf[:, k], wf[:, k], -FP8_MAX, None, ALU.max).then_inc(wf_clip, 1)
                if k >= 1:
                    dve.wait_ge(wf_hi_cut, k)
                    nc.vector.tensor_tensor(wf_lo[:, k - 1], wf[:, k - 1], wf_hi[:, k - 1].bitcast(F32), ALU.subtract).then_inc(wf_cut, 1)
            dve.wait_ge(wf_hi_cut, KT)
            nc.vector.tensor_tensor(wf_lo[:, KT - 1], wf[:, KT - 1], wf_hi[:, KT - 1].bitcast(F32), ALU.subtract).then_inc(wf_cut, 1)

            def lower(r, n):
                dve.wait_ge(t_hi, n + 1)
                dve.wait_ge(f_done, n + 1)
                nc.vector.tensor_tensor(xs_lo[:, r % 2].rearrange("p k n -> p (k n)"),
                                        bank[:, 2 * (r % 2):2 * (r % 2) + 2].rearrange("p k n -> p (k n)"),
                                        xs_hi[:, r % 2].rearrange("p k n -> p (k n)").bitcast(F32), ALU.subtract).then_inc(t_lo, 1)

            def finish(i, r, n):
                s = r % 2
                z = y2[:, s]
                dve.wait_ge(f_done, n + 3)
                dve.wait_ge(y_sent[s], i * 32 + 16 * (r // 2 + 1))
                nc.vector.scalar_tensor_tensor(out=z, in0=bank[:, 4 + 2 * s:4 + 2 * s + NH].rearrange("p a n -> p (a n)"), scalar=small[:, 19:20],
                                               in1=x1[:, r], op0=ALU.mult, op1=ALU.add).then_inc(f_read, 1)
                dve.wait_ge(f_read, n + 5)
                moments_of(z, stats2[:, s], moments2[:, s], ln2, n * LN2)
                normalise(z, moments2[:, s], ln2, n * LN2)

            lower(0, 0)
            with dve.Fori(0, TILES // 4 - 1) as i:
                for r in range(4):
                    lower(r + 1, i * 4 + r + 1)
                    finish(i, r, i * 4 + r)
            i = TILES // 4 - 1
            for r in range(4):
                if r < 3:
                    lower(r + 1, i * 4 + r + 1)
                finish(i, r, i * 4 + r)

        @block.tensor
        def _(pe):
            THREE = ((0, 0), (1, 0), (0, 1))

            pe.sem_inc(qkv_done, 2 * MT)
            pe.sem_inc(norm_done, 2)
            pe.sem_inc(s_done, 1)
            pe.sem_inc(pv_done, SLOTS)
            pe.sem_inc(den_done, 2)
            pe.sem_inc(y_done, 4)
            pe.sem_inc(t_done, 2)
            pe.sem_inc(f_done, 2)
            pe.wait_ge(consts, 8 + HG)

            def norm(tb, m):
                pe.wait_ge(sq_ready, tb * G + (m + 3))
                pe.wait_ge(norm_read, tb * G + (m + 1))
                nc.tensor.matmul(bank[:, 2 + m % 2], head_sum[:], sq[:, m % 2], start=True, stop=True).then_inc(norm_done, 1)

            with pe.Fori(0, TB // 2) as i:
                for r in range(2):
                    tb = i * 2 + r
                    for m in range(MT):
                        pe.wait_ge(w_cut, m + 1)
                        if m < G:
                            pe.wait_ge(sq_ready, tb * G + (m + 1))
                        else:
                            pe.wait_ge(raw_ready, tb * MT + 2)
                        dst = bank[:, m % 2 if m < G else KV_BANK]
                        for k in range(KT):
                            if m == 0 and k % (KT // 2) == 0:
                                pe.wait_ge(xt_cut, tb * 2 + (2 + k // (KT // 2) + 1))
                            for a, c in THREE:
                                last = nc.tensor.matmul(dst, (w_hi, w_lo)[a][:, m, k], (xt_hi[:, r], xt_lo[r])[c][:, k],
                                                        start=(k == 0 and a == c == 0), stop=(k == KT - 1 and c == 1))
                        last.then_inc(qkv_done, 1)
                        if m >= 1:
                            norm(tb, m - 1)
            pe.wait_ge(raw_ready, TB * MT + 2)
            pe.wait_ge(sq_ready, TB * G + 2)
            for tt in range(TILES):
                tb, q = tt // QT, tt % QT
                last = nc.tensor.transpose(bank[:, tt // (TILES // 2), tt % (TILES // 2) * HD:(tt % (TILES // 2) + 1) * HD],
                                           kv[SR:P, tb, q * P:(q + 1) * P], ident[SR:P, SR:P])
            last.then_inc(v_turned, 1)
            pe.wait_ge(norm_read, TB * G + 2)
            for tb in range(TB):
                pe.wait_ge(k_sq, tb + 1)
                if tb >= 2:
                    pe.wait_ge(k_norm_read, tb - 1)
                nc.tensor.matmul(bank[:, 2 + tb % 2], head_sum[0:HD, :], sq[0:HD, tb % 2], start=True, stop=True).then_inc(k_norm_done, 1)

            pe.wait_ge(flag_ready, 1)
            needed = pe.value_load(flag[0:1, 0:1], min_val=0, max_val=1)
            with pe.If(needed == 1):
                pe.sem_inc(m_turned, 2)
                with pe.Fori(0, B) as b:
                    wait_apart(pe, m_k_in, b * 16 + 16)
                    with pe.Fori(0, H // 2) as hp:
                        for r in range(2):
                            n = b * H + r + hp * 2
                            pe.wait_ge(m_q_in[r], b * (48 * H // 2) + hp * 48 + 48)
                            for q in range(TT):
                                pe.wait_ge(m_s_read, n * TT + (q + 1))
                                if q == 0:
                                    pe.wait_ge(m_lo_cut, n + 1)
                                queries = q_m[:, r, q * P:(q + 1) * P]
                                for c in range(q // 4 + 1):
                                    own = c == q // 4
                                    width = (q % 4 + 1) * P if own else 512
                                    dst = bank[:, 4 * (q % 2) + c]
                                    nc.tensor.matmul(dst[:, 0:width], queries, k_m[:, c * 512:c * 512 + width], start=True, stop=not own)
                                    if own:
                                        last = nc.tensor.matmul(dst[:, width - P:width], ident_bf[:], mask_bf[:], start=False, stop=True)
                                last.then_inc(m_s_done, 1)
                            pe.wait_ge(m_s_read, n * TT + (TT + 2))
                            nc.tensor.transpose(bank[0:TT, 0, 0:P], row_max[:], ident[:]).then_inc(m_turned, 1)

            pe.wait_ge(fixed, 2)

            def half_projection(hi, lo, half, y_bank, part, parts):
                todo = [(k, a, c) for k in range(KT) for a, c in THREE]
                cols = slice(half * 512, (half + 1) * 512)
                for i in range(len(todo) * part // parts, len(todo) * (part + 1) // parts):
                    k, a, c = todo[i]
                    last = nc.tensor.matmul(bank[:, y_bank], (hi, lo)[a][:, k], (wo_hi, wo_lo)[c][:, k, cols],
                                            start=(i == 0), stop=(i == len(todo) - 1), skip_group_check=True)
                if part == parts - 1:
                    last.then_inc(y_done, 1)

            with pe.Fori(0, B) as b:
                def scores(s0, j, slot, t):
                    off = first_query(j, t)
                    for p in range(2):
                        pe.wait_ge(p_done, s0 * 2 + (2 * t + p + 1))
                        for h in (2 * p, 2 * p + 1):
                            last = nc.tensor.matmul(bank[:, h, off:NB], k_st[:, t * P:(t + 1) * P], q_st[:, slot, h, off:NB], start=True, stop=True)
                        last.then_inc(s_done, 1)

                def denominators(n, r):
                    pe.wait_ge(den_read, n + 1)
                    for h in range(HG):
                        last = nc.tensor.matmul(bank[h * HD:(h + 1) * HD, DEN_BANK], ones[:], acc[:, r, h], start=True, stop=True)
                    last.then_inc(den_done, 1)

                wait_apart(pe, kv_in, b * 32 + 32)
                pe.wait_ge(q_in, b * (SEQ_GROUPS * 64) + 64)
                scores(b * SEQ_STEPS, 0, 0, 0)

                def body(j, gp, first, last_pair):
                    NT = key_tiles(j)
                    for r in range(2):
                        n, s0 = group(b, j, gp, r), step(b, j, gp, r)
                        for t in range(NT):
                            if t + 1 < NT:
                                scores(s0, j, r, t + 1)
                            elif not (last_pair and r == 1):
                                pe.wait_ge(q_in, n * 64 + 128)
                                scores(s0 + NT, 0, 1 - r, 0)
                            off = first_query(j, t)
                            if t == 0:
                                pe.wait_ge(att_ready, n + 1)
                            pe.wait_ge(p_done, s0 * 2 + (2 * t + 4))
                            if t >= QT * j:
                                pe.wait_ge(masked, n * QT + (t - QT * j + 1))
                            for h in range(HG):
                                last = nc.tensor.matmul(bank[h * HD:(h + 1) * HD, 4 + r, off:NB], v_sb[:, t], prob[:, t % SLOTS, h, off:NB],
                                                        start=(t == 0), stop=(t == NT - 1), skip_group_check=True)
                            last.then_inc(pv_done, 1)
                            if t == 1 and not (first and r == 0):
                                pe.wait_ge(acc_done, s0 + SLOTS)
                                denominators(n - 1, 1 - r)
                            if j > 0 and t in (window := projection_steps(j, r)):
                                if t == window[0]:
                                    tile = projected(b, j, gp)
                                    pe.wait_ge(att_cut, tile + 1)
                                    pe.wait_ge(y_read, tile * 2 + (r + 2))
                                half_projection(att_hi, att_lo, r, Y_BANK, t - window[0], len(window))

                pairs_of_groups(pe, b, body)
                pe.wait_ge(acc_done, (b + 1) * SEQ_STEPS + SLOTS)
                denominators(b * SEQ_GROUPS + (SEQ_GROUPS - 1), 1)
                for t in range(QT):
                    tile = projected(b, JB, t)
                    pe.wait_ge(att_cut, tile + 1)
                    for half in range(2):
                        if t == 0 and half == 0:
                            pe.wait_ge(y_read, tile * 2 + 2)
                            pe.wait_ge(den_read, b * SEQ_GROUPS + (SEQ_GROUPS + 1))
                        elif t >= 1:
                            pe.wait_ge(y_read, tile * 2 + (half + 1))
                        half_projection(end_hi[:, t % 2], end_lo[:, t % 2], half, Y_BANK - half, 0, 1)

            def turn(r, n):
                pe.wait_ge(sim_ready, n * 2 + 2)
                pe.wait_ge(t_lo, n + 1)
                for k in range(KT):
                    last = nc.tensor.transpose(bank[:, 2 * (r % 2) + k // 4, (k % 4) * P:(k % 4 + 1) * P], x_sim[:, r % 2, k * P:(k + 1) * P], ident[:])
                last.then_inc(t_done, 1)

            def product(r, n):
                pe.wait_ge(t_lo, n + 3)
                pe.wait_ge(f_read, n + 3)
                for h in range(NH):
                    cols = slice(h * 512, (h + 1) * 512)
                    for k in range(KT):
                        pe.wait_ge(wf_cut, k + 1)
                        for a, c in THREE:
                            last = nc.tensor.matmul(bank[:, 4 + 2 * (r % 2) + h], (xs_hi, xs_lo)[a][:, r % 2, k], (wf_hi, wf_lo)[c][:, k, cols],
                                                    start=(k == 0 and a == c == 0), stop=(k == KT - 1 and c == 1))
                last.then_inc(f_done, 1)

            pe.wait_ge(y_read, 2 * TILES + 2)
            turn(0, 0)
            with pe.Fori(0, TILES // 4 - 1) as i:
                for r in range(4):
                    turn(r + 1, i * 4 + r + 1)
                    product(r, i * 4 + r)
            i = TILES // 4 - 1
            for r in range(4):
                if r < 3:
                    turn(r + 1, i * 4 + r + 1)
                product(r, i * 4 + r)

    return nc


HEADS = 32


def kernel(L0_attn_x, L0_attn_wq_w, L0_attn_wq_b, L0_attn_wk_w, L0_attn_wk_b, L0_attn_wv_w, L0_attn_wv_b,
           L0_attn_wo_w, L0_attn_wo_b, L0_ffn_weight):
    import numpy as np
    import concourse.bacc as bacc
    from concourse.bass_utils import run_bass_kernel_spmd

    x = np.ascontiguousarray(L0_attn_x)
    B, T, D = x.shape
    kt = D // P

    def by_partition(w):
        return np.ascontiguousarray(w.reshape(kt, P, -1).transpose(1, 0, 2))

    flat = x.reshape(B * T, D)
    blocks = flat.reshape(-1, 512, kt, P).transpose(0, 3, 2, 1)
    w_qkv = np.concatenate([np.asarray(w) for w in (L0_attn_wq_w, L0_attn_wk_w, L0_attn_wk_w, L0_attn_wk_w, L0_attn_wv_w)]).T
    b_qkv = np.concatenate([np.asarray(w) for w in (L0_attn_wq_b, L0_attn_wk_b, L0_attn_wk_b, L0_attn_wk_b, L0_attn_wv_b)])
    arrays = {
        "x_t": np.ascontiguousarray(blocks),
        "x": flat,
        "w_qkv": np.ascontiguousarray(w_qkv.reshape(kt, P, -1, P).transpose(1, 2, 0, 3)),
        "b_qkv": np.ascontiguousarray(b_qkv.reshape(-1, P).T),
        "w_o": by_partition(np.asarray(L0_attn_wo_w).T),
        "b_o": np.ascontiguousarray(np.broadcast_to(np.asarray(L0_attn_wo_b), (P, D))),
        "w_f": by_partition(np.asarray(L0_ffn_weight)),
    }
    nc = bacc.Bacc("TRN2", target_bir_lowering=False, num_devices=1)
    aps = {n: nc.dram_tensor(n, a.shape, mybir.dt.from_np(a.dtype), kind="ExternalInput").ap() for n, a in arrays.items()}
    out = nc.dram_tensor("out", (B * T, D), F32, kind="ExternalOutput").ap()
    build(nc, out=out, B=B, T=T, H=HEADS, **aps)
    r = run_bass_kernel_spmd(nc, [arrays], core_ids=[0])
    return r.results[0]["out"].reshape(B, T, D)
```

```python
from contextlib import ExitStack

import concourse.bass as bass
from concourse import mybir

F32 = mybir.dt.float32
F32R = mybir.dt.float32r
BF16 = mybir.dt.bfloat16
I32 = mybir.dt.int32
ALU = mybir.AluOpType
ACT = mybir.ActivationFunctionType
AX = mybir.AxisListType
RMAX = bass.bass_isa.ReduceOp.max

P = 128
FP8_MAX = 448.0
SCALE_EPS = 1e-12
LN_EPS = 1e-5
EXP_SAFE = 60.0
MASKED = -3.0e38


def build(nc, x_t, x, w_qkv, b_qkv, w_o, b_o, w_f, out, B, T, H):
    D = x.shape[1]
    HD = D // H
    KT = D // P
    NB = 512
    TB = B * T // NB
    JB = T // NB
    QT = NB // P
    TT = T // P
    TILES = B * TT
    HG = P // HD
    G = H // HG
    MT = G + 1
    NH = D // 512
    SR = 3 * HD
    SM = SR + 2
    SCALE = float(HD) ** -0.5
    SAFE_NORMS = (EXP_SAFE / SCALE) ** 2
    SLOTS = QT
    REPS = HD // HG
    FIXED = 4 + HG
    LN = 7
    LN2 = 6
    assert KT == B * G // 2
    assert HG == 4 and NH == 2 and TB == KT and G == 2 * QT and JB % 2 == 0 and TILES % 4 == 0

    q_hi_d = nc.dram_tensor("q_hi_d", (TB, H * HD, NB), F32).ap()
    q_lo_d = nc.dram_tensor("q_lo_d", (TB, H * HD, NB), F32).ap()
    k_st_d = nc.dram_tensor("k_st_d", (TB, SR, NB), F32).ap()
    v_d = nc.dram_tensor("v_d", (TB, P, QT, HD), F32).ap()
    max_d = nc.dram_tensor("max_d", (2, TB, H, NB), F32).ap()
    wf_sim_d = nc.dram_tensor("wf_sim_d", (P, KT, D), F32).ap()
    x1_d = nc.dram_tensor("x1_d", (TILES, P, D), F32).ap()
    x_tiles = x.rearrange("(n p) d -> n p d", p=P)
    out_tiles = out.rearrange("(n p) d -> n p d", p=P)

    ctx = ExitStack()

    def sem(name):
        return ctx.enter_context(nc.semaphore(name))

    with ctx:
        def sb(name, shape, dt=F32, stack=ctx):
            return stack.enter_context(nc.sbuf_tensor(name, shape, dt))

        ident = sb("ident", [P, P])
        ident_bf = sb("ident_bf", [P, P], BF16)
        mask_bf = sb("mask_bf", [P, P], BF16)
        amax_x = sb("amax_x", [P, TILES])
        amax_w = sb("amax_w", [P, KT])
        small = sb("small", [P, 32])
        exponent = sb("exponent", [P, 1])
        flag = sb("flag", [P, 1], I32)

        with ExitStack() as s:
            w_hi = sb("w_hi", [P, MT, KT, P], F32R, s)
            w_lo = sb("w_lo", [P, MT, KT, P], F32R, s)
            xt_raw = sb("xt_raw", [P, KT, NB], F32, s)
            xt_hi = sb("xt_hi", [P, 2, KT, NB], F32R, s)
            xt_lo0 = sb("xt_lo0", [P, KT, NB], F32R, s)
            with ExitStack() as s_stage:
                w_stage = sb("w_stage", [P, 2, KT, P], F32, s_stage)
            xt_lo1 = sb("xt_lo1", [P, KT, NB], F32R, s)
            kv = sb("kv", [P, TB, NB], F32, s)
            bias = sb("bias", [P, MT], F32, s)
            head_sum = sb("head_sum", [P, P], F32R, s)
            raw = sb("raw", [P, 2, NB], F32, s)
            sq = sb("sq", [P, 2, NB], F32R, s)
            part_hi = sb("part_hi", [P, 2, NB], F32R, s)
            part_lo = sb("part_lo", [P, 2, NB], F32R, s)
            wf_tile = sb("wf_tile", [P, D], F32, s)
            v_t = sb("v_t", [P, TB, QT, HD], F32, s)
            norms = sb("norms", [P, TB, MT], F32, s)
            centre = sb("centre", [P, B], F32, s)
            centre_part = sb("centre_part", [P, TB], F32, s)
            zeros = sb("zeros", [P, NB], F32, s)
            xt_lo = (xt_lo0, xt_lo1)
            wo_stage = xt_raw[:].rearrange("p (s a) n -> p s (a n)", s=4)
            k_hi = xt_hi[:, :, 0:JB]
            k_lo = [lo[:, 0:JB] for lo in xt_lo]

        with ExitStack() as s:
            wo_hi = sb("wo_hi", [P, KT, D], F32R, s)
            bo = sb("bo", [P, D], F32, s)
            wo_lo = sb("wo_lo", [P, KT, D], F32R, s)
            res = sb("res", [P, D], F32, s)
            with ExitStack() as s_maxima:
                q_m = sb("q_m", [SR, 2, T], F32R, s_maxima)
                k_m = sb("k_m", [SR, T], F32R, s_maxima)
                row_max = sb("row_max", [P, TT], F32, s_maxima)
                max_hi = sb("max_hi", [TT, P], F32R, s_maxima)
                max_lo = sb("max_lo", [TT, P], F32R, s_maxima)
            k_st = sb("k_st", [SM, T], F32R, s)
            v_sb = sb("v_sb", [P, TT, HD], F32, s)
            q_st = sb("q_st", [SM, 2, HG, NB], F32R, s)
            acc = sb("acc", [P, 2, HG, NB], F32, s)
            att = sb("att", [P, 2 * G, NB], F32, s)
            with ExitStack() as s_prob:
                prob = sb("prob", [P, SLOTS, HG, NB], F32, s_prob)
            with ExitStack() as s_end:
                end_res = sb("end_res", [P, QT, D], F32, s_end)
                end_hi = sb("end_hi", [P, 2, KT, P], F32R, s_end)
                end_lo = sb("end_lo", [P, 2, KT, P], F32R, s_end)
            s.enter_context(nc.sbuf_tensor("prob_place", [P, SLOTS, HG, NB], F32))
            head_col = sb("head_col", [P, HG, HD], F32, s)
            spread = sb("spread", [P, QT, P], F32, s)
            r_den = sb("r_den", [P, P], F32, s)
            wf_piece = sb("wf_piece", [P, D], F32, s)
            att_hi = sb("att_hi", [P, KT, P], F32R, s)
            att_lo = sb("att_lo", [P, KT, P], F32R, s)
            stats = sb("stats", [P, 2, NH, 6], F32, s)
            moments = sb("moments", [P, 2, 4], F32, s)

        with ExitStack() as s:
            wf_hi = sb("wf_hi", [P, KT, D], F32R, s)
            s.enter_context(nc.sbuf_tensor("bo_place", [P, D], F32))
            wf_lo = sb("wf_lo", [P, KT, D], F32R, s)
            s.enter_context(nc.sbuf_tensor("res_place", [P, D], F32))
            wf = sb("wf", [P, KT, D], F32, s)
            x1 = sb("x1", [P, 4, D], F32, s)
            x_sim = sb("x_sim", [P, 2, D], F32, s)
            xs_hi = sb("xs_hi", [P, 2, KT, P], F32R, s)
            xs_lo = sb("xs_lo", [P, 2, KT, P], F32R, s)
            y2 = sb("y2", [P, 2, D], F32, s)
            stats2 = sb("stats2", [P, 2, NH, 6], F32, s)
            moments2 = sb("moments2", [P, 2, 4], F32, s)

        bank = ctx.enter_context(nc.psum_tensor("bank", [P, 8, 512], F32))
        Y_BANK, DEN_BANK, KV_BANK = 7, 6, 6

        consts = sem("consts")
        passed = sem("passed")
        w_in = [sem("w_in0"), sem("w_in1")]
        w_hi_cut, w_cut = sem("w_hi_cut"), sem("w_cut")
        b_in = sem("b_in")
        zeros_sent = sem("zeros_sent")
        xt_in = sem("xt_in")
        xt_hi_cut, xt_cut = sem("xt_hi_cut"), sem("xt_cut")
        wf_tile_in = sem("wf_tile_in")
        wf_tile_read = sem("wf_tile_read")
        qkv_done = sem("qkv_done")
        raw_ready = sem("raw_ready")
        sq_ready = sem("sq_ready")
        norm_done = sem("norm_done")
        norm_read = sem("norm_read")
        hi_cut = sem("hi_cut")
        lo_cut = sem("lo_cut")
        part_sent = [sem("part_sent0"), sem("part_sent1")]
        k_summed = sem("k_summed")
        centred = sem("centred")
        k_cut = sem("k_cut")
        v_copied = sem("v_copied")
        k_sq = sem("k_sq")
        k_norm_done = sem("k_norm_done")
        k_norm_read = sem("k_norm_read")
        v_turned = sem("v_turned")
        kv_sent = sem("kv_sent")
        bound_steps = sem("bound_steps")
        bound_all = sem("bound_all")
        flag_ready = sem("flag_ready")
        project_over = sem("project_over")

        m_k_in = sem("m_k_in")
        m_q_in = [sem("m_q_in0"), sem("m_q_in1")]
        m_s_done = sem("m_s_done")
        m_s_read = sem("m_s_read")
        m_turned = sem("m_turned")
        m_hi_cut, m_lo_cut = sem("m_hi_cut"), sem("m_lo_cut")
        m_sent = sem("m_sent")
        attend_go = sem("attend_go")

        wo_in = [sem(f"wo_in{i}") for i in range(4)]
        wo_hi_cut, wo_cut = sem("wo_hi_cut"), sem("wo_cut")
        bo_in = sem("bo_in")
        fixed = sem("fixed")
        kv_in = sem("kv_in")
        q_in = sem("q_in")
        s_done = sem("s_done")
        p_done = sem("p_done")
        masked = sem("masked")
        pv_done = sem("pv_done")
        acc_done = sem("acc_done")
        den_done = sem("den_done")
        den_read = sem("den_read")
        spread_done = sem("spread_done")
        pv_moved = sem("pv_moved")
        att_ready = sem("att_ready")
        att_hi_cut = sem("att_hi_cut")
        att_cut = sem("att_cut")
        y_done = sem("y_done")
        y_read = sem("y_read")
        res_in = sem("res_in")
        end_in = [sem(f"end_in{t}") for t in range(QT)]
        res_ready = sem("res_ready")
        ln1 = sem("ln1")
        x1_sent = sem("x1_sent")
        end_sent = sem("end_sent")

        piece_in = sem("piece_in")
        piece_clip = sem("piece_clip")
        piece_sent = sem("piece_sent")
        wf_in = [sem(f"wf_in{k}") for k in range(KT)]
        scale_steps = sem("scale_steps")
        wf_hi_cut, wf_cut = sem("wf_hi_cut"), sem("wf_cut")
        g_all = sem("g_all")
        x1_in = [sem(f"x1_in{i}") for i in range(4)]
        sim_ready = sem("sim_ready")
        t_done = sem("t_done")
        t_hi = sem("t_hi")
        t_lo = sem("t_lo")
        f_done = sem("f_done")
        f_read = sem("f_read")
        ln2 = sem("ln2")
        y_sent = [sem("y_sent0"), sem("y_sent1")]

        SEQ_STEPS = G * QT * JB * (JB + 1) // 2
        SEQ_GROUPS = JB * G

        def key_tiles(j):
            return QT * (j + 1)

        def group(b, j, gp, r):
            return b * SEQ_GROUPS + (j * G + r) + gp * 2

        def step(b, j, gp, r):
            n = key_tiles(j)
            return b * SEQ_STEPS + (G * QT * j * (j + 1) // 2 + r * n) + gp * (2 * n)

        def projected(b, j, gp):
            return b * TT + (j - 1) * QT + gp

        def stored_alone(b, j, gp):
            return b * (TT - QT) + (j - 1) * QT + gp

        def first_query(j, t):
            return P * max(0, t - QT * j)

        def pairs_of_groups(eng, b, body):
            for j in range(JB):
                first, last = int(j == 0), int(j == JB - 1)
                if first:
                    body(j, 0, True, False)
                with eng.Fori(first, G // 2 - last) as gp:
                    body(j, gp, False, False)
                if last:
                    body(j, G // 2 - 1, False, True)

        def group_before(j, gp, r):
            at = (gp * 2 + (j % 2 * G + r + 2 * G - 1)) % (2 * G)
            return one(att[:, bass.ds(at, 1)])

        def projection_steps(j, r):
            half = key_tiles(j) // 2
            return range(half + 1, 2 * half) if r == 0 else range(4, min(half + 4, 2 * half - 1))

        def wait_apart(eng, semaphore, value):
            eng.wait_ge(semaphore, value)
            eng.sem_inc(passed, 1)

        def one(ap):
            return ap.rearrange("p a n -> p (a n)")

        def flat(ap):
            return ap.rearrange("p k n -> p (k n)")

        block = ctx.enter_context(nc.Block())

        @block.sync
        def _(sp):
            sp.dma_start(bias[:], b_qkv).then_inc(b_in, 16)

            def load_w(m):
                if m >= 2:
                    sp.wait_ge(w_cut, m - 1)
                sp.dma_start(w_stage[:, m % 2], w_qkv[:, m]).then_inc(w_in[m % 2], 16)

            load_w(0)
            for half in range(2):
                k = slice(half * KT // 2, (half + 1) * KT // 2)
                sp.dma_start(xt_raw[:, k], x_t[0, :, k]).then_inc(xt_in, 16)
                sp.wait_ge(xt_in, 16 * (half + 1))
            for m in range(1, MT):
                load_w(m)
            sp.dma_start(wf_tile[:], w_f[:, 0]).then_inc(wf_tile_in, 16)
            with sp.Fori(1, TB) as tb:
                for half in range(2):
                    k = slice(half * KT // 2, (half + 1) * KT // 2)
                    sp.wait_ge(xt_cut, tb * 2 + (half + 1))
                    sp.dma_start(xt_raw[:, k], x_t[bass.ds(tb, 1), :, k].rearrange("a p k n -> p (a k) n")).then_inc(xt_in, 16)
                    wait_apart(sp, xt_in, tb * 32 + 16 * (half + 1))
                sp.wait_ge(wf_tile_read, tb + 1)
                sp.dma_start(wf_tile[:], one(w_f[:, bass.ds(tb, 1)])).then_inc(wf_tile_in, 16)

            sp.wait_ge(xt_cut, 2 * TB + 2)
            for k in range(KT):
                if k >= 4:
                    sp.wait_ge(wo_cut, k - 3)
                sp.dma_start(wo_stage[:, k % 4], w_o[:, k]).then_inc(wo_in[k % 4], 16)
            for s in part_sent:
                sp.wait_ge(s, 32 * (TB * G // 2 + 1))
            sp.wait_ge(kv_sent, 16 * (2 * B + TB))
            sp.wait_ge(zeros_sent, 32 * H * TB // P)
            sp.wait_ge(flag_ready, 1)
            sp.wait_ge(wo_cut, KT)
            sp.sem_inc(project_over, 1)

            needed = sp.value_load(flag[0:1, 0:1], min_val=0, max_val=1)
            with sp.If(needed == 1):
                q_hi_m = q_hi_d.rearrange("t (h p) n -> h p t n", p=HD)
                q_lo_m = q_lo_d.rearrange("t (h p) n -> h p t n", p=HD)
                with sp.Fori(0, B) as b:
                    blocks = bass.ds(b * JB, JB)
                    sp.wait_ge(m_turned, b * H + 2)
                    sp.dma_start(k_m[:].bitcast(F32).rearrange("r (t n) -> r t n", n=NB), k_st_d[blocks].rearrange("t r n -> r t n")).then_inc(m_k_in, 16)
                    with sp.Fori(0, H // 2) as hp:
                        for r in range(2):
                            n = b * H + r + hp * 2
                            head = bass.ds(hp * 2 + r, 1)
                            sp.wait_ge(m_turned, n + 1)
                            for rows, src in ((0, q_hi_m), (HD, q_lo_m), (2 * HD, q_hi_m)):
                                sp.dma_start(q_m[rows:rows + HD, r].bitcast(F32).rearrange("p (t n) -> p t n", n=NB),
                                             src[head, :, blocks].rearrange("a p t n -> (a p) t n")).then_inc(m_q_in[r], 16)
                sp.wait_ge(m_sent, 32 * JB * (B * H + 1))
            sp.sem_inc(attend_go, 1)

            q_hi_h = q_hi_d.rearrange("t (h p) n -> (t h) p n", p=HD)
            q_lo_h = q_lo_d.rearrange("t (h p) n -> (t h) p n", p=HD)
            max_h = max_d.rearrange("c t h n -> c (t h) n")

            def load_q(n, slot):
                heads = bass.ds(n * HG, HG)
                sp.dma_start(q_st[0:HD, slot].bitcast(F32), q_hi_h[heads].rearrange("h p n -> p h n")).then_inc(q_in, 16)
                sp.dma_start(q_st[HD:2 * HD, slot].bitcast(F32), q_lo_h[heads].rearrange("h p n -> p h n")).then_inc(q_in, 16)
                sp.dma_start(q_st[2 * HD:SR, slot].bitcast(F32), q_hi_h[heads].rearrange("h p n -> p h n")).then_inc(q_in, 16)
                sp.dma_start(q_st[SR:SM, slot].bitcast(F32), max_h[:, heads]).then_inc(q_in, 16)
                wait_apart(sp, q_in, n * 64 + 64)

            with sp.Fori(0, B) as b:
                sp.wait_ge(den_done, b * SEQ_GROUPS + 2)
                blocks = bass.ds(b * JB, JB)
                sp.dma_start(k_st[0:SR].bitcast(F32).rearrange("r (t n) -> r t n", n=NB), k_st_d[blocks].rearrange("t r n -> r t n")).then_inc(kv_in, 16)
                sp.dma_start(v_sb[:].rearrange("p (t q) d -> p t (q d)", q=QT), v_d[blocks].rearrange("t p q d -> p t (q d)")).then_inc(kv_in, 16)
                load_q(b * SEQ_GROUPS, 0)

                def body(j, gp, first, last):
                    if j == 0:
                        piece = b * (G // 2) + gp
                        sp.wait_ge(piece_sent, piece * 16 + 16)
                        sp.dma_start(wf_piece[:], one(w_f[:, bass.ds(piece, 1)])).then_inc(piece_in, 16)
                    if j > 0:
                        tile = projected(b, j, gp)
                        sp.wait_ge(x1_sent, stored_alone(b, j, gp) * 16 + 16)
                        sp.wait_ge(ln1, tile * LN + LN)
                        sp.dma_start(res[:], x_tiles[bass.ds(tile, 1)].rearrange("a p d -> p (a d)")).then_inc(res_in, 16)
                    for r in range(2):
                        if not (last and r == 1):
                            sp.wait_ge(s_done, step(b, j, gp, r) * 2 + 1)
                            load_q(group(b, j, gp, r) + 1, 1 - r)
                        if j == 0 and r == 0:
                            sp.wait_ge(piece_clip, piece * 2 + 2)
                            sp.dma_start(one(wf_sim_d[:, bass.ds(piece, 1)]), wf_piece[:]).then_inc(piece_sent, 16)
                    if j > 0:
                        sp.wait_ge(ln1, tile * LN + (LN + 6))
                        sp.dma_start(x1_d[bass.ds(tile, 1)].rearrange("a p d -> p (a d)"), res[:]).then_inc(x1_sent, 16)

                pairs_of_groups(sp, b, body)
                for t in range(QT):
                    tile = projected(b, JB, t)
                    if t == 0:
                        sp.wait_ge(pv_done, (b + 1) * SEQ_STEPS + SLOTS)
                        sp.wait_ge(acc_done, (b + 1) * SEQ_STEPS + SLOTS)
                    sp.dma_start(end_res[:, t], x_tiles[bass.ds(tile, 1)].rearrange("a p d -> p (a d)")).then_inc(end_in[t], 16)

            sp.wait_ge(den_done, B * SEQ_GROUPS + 2)
            sp.wait_ge(piece_sent, 16 * (KT + 1))
            for k in range(KT):
                sp.dma_start(wf[:, k], wf_sim_d[:, k]).then_inc(wf_in[k], 16)
            sp.wait_ge(x1_sent, 16 * (TILES - B * QT + 1))
            for r in range(4):
                sp.dma_start(x1[:, r], x1_d[r]).then_inc(x1_in[r], 16)
            sp.wait_ge(end_sent, 16 * QT * (B + 1))
            with sp.Fori(1, TILES // 4) as i:
                for r in range(4):
                    sp.wait_ge(f_read, i * 4 + r + 1)
                    sp.dma_start(x1[:, r], x1_d[bass.ds(i * 4 + r, 1)].rearrange("a p d -> p (a d)")).then_inc(x1_in[r], 16)
            for i in range(2):
                sp.wait_ge(y_sent[i], 16 * (TILES // 2 + 1))

        @block.gpsimd
        def _(pool):
            pool.sem_inc(xt_cut, 2)
            nc.gpsimd.memset(ident[:], 0.0).then_inc(consts, 1)
            nc.gpsimd.memset(mask_bf[:], 0.0).then_inc(consts, 1)
            nc.gpsimd.memset(head_sum[:].bitcast(F32), 0.0).then_inc(consts, 1)
            nc.gpsimd.memset(zeros[:], 0.0).then_inc(consts, 1)
            nc.gpsimd.memset(exponent[:], -0.5).then_inc(consts, 1)
            pool.wait_ge(consts, 5)
            nc.gpsimd.affine_select(out=ident[:], in_=ident[:], compare_op=ALU.not_equal, fill=1.0,
                                    base=0, pattern=[[-1, P]], channel_multiplier=1).then_inc(consts, 1)
            nc.gpsimd.affine_select(out=mask_bf[:], in_=mask_bf[:], compare_op=ALU.is_ge, fill=MASKED,
                                    base=0, pattern=[[-1, P]], channel_multiplier=1).then_inc(consts, 1)
            for h in range(HG):
                pool.wait_ge(consts, 7 + h)
                nc.gpsimd.memset(head_sum[h * HD:(h + 1) * HD, h * HD:(h + 1) * HD].bitcast(F32), 1.0).then_inc(consts, 1)
            pool.wait_ge(consts, 7 + HG)
            nc.gpsimd.tensor_copy(ident_bf[:], ident[:]).then_inc(consts, 1)

            def inverse_deviation(moments, done, before):
                wait_apart(pool, done, before + (NH + 1))
                nc.gpsimd.tensor_scalar(moments[:, 1:2], moments[:, 1:2], LN_EPS, None, ALU.add).then_inc(done, 1)
                wait_apart(pool, done, before + (NH + 2))
                nc.gpsimd.tensor_tensor(moments[:, 2:3], moments[:, 1:2], exponent[:], ALU.pow).then_inc(done, 1)

            def cut_x(i, r):
                tb = i * 2 + r
                wait_apart(pool, qkv_done, tb * MT + MT)
                if r == 1:
                    pool.wait_ge(w_cut, MT)
                for half in range(2):
                    k = slice(half * KT // 2, (half + 1) * KT // 2)
                    u = tb * 2 + half
                    wait_apart(pool, xt_in, u * 16 + 16)
                    nc.gpsimd.tensor_copy(xt_hi[:, r, k], xt_raw[:, k]).then_inc(xt_hi_cut, 1)
                    pool.wait_ge(xt_hi_cut, u + 1)
                    nc.gpsimd.tensor_tensor(xt_lo[r][:, k], xt_raw[:, k], xt_hi[:, r, k].bitcast(F32), ALU.subtract).then_inc(xt_cut, 1)

            cut_x(0, 1)
            with pool.Fori(1, TB // 2) as i:
                for r in range(2):
                    cut_x(i, r)
            for k in range(KT // 2):
                pool.wait_ge(wo_hi_cut, k + 1)
                nc.gpsimd.tensor_tensor(wo_lo[:, k], wo_stage[:, k % 4], wo_hi[:, k].bitcast(F32), ALU.subtract).then_inc(wo_cut, 1)
            pool.wait_ge(bound_steps, 4)
            nc.gpsimd.partition_all_reduce(small[:, 3:6], small[:, 0:3], P, RMAX).then_inc(bound_all, 1)

            pool.wait_ge(attend_go, 1)
            nc.gpsimd.memset(k_st[SR:SM].bitcast(F32), -1.0).then_inc(fixed, 1)
            pool.wait_ge(fixed, 1)
            nc.gpsimd.memset(head_col[:], 0.0).then_inc(fixed, 1)
            nc.gpsimd.memset(spread[:], 0.0).then_inc(fixed, 1)
            pool.wait_ge(fixed, 3)
            for h in range(HG):
                nc.gpsimd.memset(head_col[:, h, h * REPS:(h + 1) * REPS], 1.0).then_inc(fixed, 1)
            nc.gpsimd.affine_select(out=spread[:].rearrange("p c (h d) -> p (c h) d", d=HD), in_=spread[:].rearrange("p c (h d) -> p (c h) d", d=HD),
                                    compare_op=ALU.not_equal, fill=1.0, base=0, pattern=[[-REPS, QT * HG], [0, HD]], channel_multiplier=1).then_inc(fixed, 1)
            pool.wait_ge(fixed, FIXED)
            pool.wait_ge(bo_in, 16)
            with pool.Fori(0, B) as b:
                def body(j, gp, first, last):
                    if j > 0:
                        tile = projected(b, j, gp)
                        wait_apart(pool, att_hi_cut, tile + 1)
                        heads = att[:, (j - 1) % 2 * G:(j - 1) % 2 * G + G, bass.ds(gp * P, P)]
                        nc.gpsimd.tensor_tensor(att_lo[:], heads, att_hi[:].bitcast(F32), ALU.subtract).then_inc(att_cut, 1)
                    for r in range(2):
                        n, s0 = group(b, j, gp, r), step(b, j, gp, r)
                        for i in range(QT):
                            t = QT * j + i
                            off = first_query(j, t)
                            wait_apart(pool, p_done, s0 * 2 + (2 * t + 4))
                            tri = prob[:, t % SLOTS, :, off:off + P]
                            nc.gpsimd.affine_select(out=tri, in_=tri, compare_op=ALU.is_ge, fill=0.0, base=0,
                                                    pattern=[[0, HG], [1, P]], channel_multiplier=-1).then_inc(masked, 1)
                        if j > 0 and r == 0:
                            pool.wait_ge(res_in, stored_alone(b, j, gp) * 16 + 16)
                            nc.gpsimd.tensor_tensor(res[:], res[:], bo[:], ALU.add).then_inc(res_ready, 1)
                    if j > 0:
                        inverse_deviation(moments[:, 0], ln1, tile * LN + LN)

                pairs_of_groups(pool, b, body)
                for t in range(QT):
                    tile = projected(b, JB, t)
                    pool.wait_ge(att_hi_cut, tile + 1)
                    heads = att[:, (JB - 1) % 2 * G:(JB - 1) % 2 * G + G, t * P:(t + 1) * P]
                    nc.gpsimd.tensor_tensor(end_lo[:, t % 2], heads, end_hi[:, t % 2].bitcast(F32), ALU.subtract).then_inc(att_cut, 1)
                    pool.wait_ge(end_in[t], b * 16 + 16)
                    nc.gpsimd.tensor_tensor(end_res[:, t], end_res[:, t], bo[:], ALU.add).then_inc(res_ready, 1)
                    if t >= 1:
                        inverse_deviation(moments[:, (t - 1) % 2], ln1, (tile - 1) * LN + LN)
                inverse_deviation(moments[:, (QT - 1) % 2], ln1, projected(b, JB, QT - 1) * LN + LN)

            pool.wait_ge(scale_steps, 1)
            nc.gpsimd.partition_all_reduce(small[:, 9:10], small[:, 8:9], P, RMAX).then_inc(g_all, 1)
            pool.wait_ge(scale_steps, 4)
            pool.wait_ge(sim_ready, 2)

            def clip(i, r):
                n = i * 4 + r
                pool.wait_ge(x1_in[r % 4], i * 16 + 16 * (r // 4 + 1))
                wait_apart(pool, t_done, n + 1)
                nc.gpsimd.tensor_scalar(x_sim[:, r % 2], x1[:, r % 4], small[:, 14:15], FP8_MAX, ALU.mult, ALU.min).then_inc(sim_ready, 1)
                wait_apart(pool, sim_ready, n * 2 + 1)
                nc.gpsimd.tensor_scalar(x_sim[:, r % 2], x_sim[:, r % 2], -FP8_MAX, None, ALU.max).then_inc(sim_ready, 1)

            clip(0, 1)
            with pool.Fori(0, TILES // 4 - 1) as i:
                for r in range(4):
                    clip(i, r + 2)
                    inverse_deviation(moments2[:, r % 2], ln2, (i * 4 + r) * LN2)
            i = TILES // 4 - 1
            for r in range(4):
                if r < 2:
                    clip(i, r + 2)
                inverse_deviation(moments2[:, r % 2], ln2, (i * 4 + r) * LN2)

        @block.scalar
        def _(act):
            act.sem_inc(raw_ready, 2)
            act.sem_inc(sq_ready, 2)
            act.sem_inc(p_done, 2)
            act.sem_inc(pv_moved, 2)
            for s in part_sent:
                act.sem_inc(s, 32)
            act.sem_inc(end_sent, 16 * QT)
            for s in (x1_sent, piece_sent, *y_sent):
                act.sem_inc(s, 16)
            act.wait_ge(consts, 5)
            for c in range(2):
                for i in range(TB * H // P):
                    act.dma_start(max_d[c].rearrange("t h n -> (t h) n")[i * P:(i + 1) * P], zeros[:]).then_inc(zeros_sent, 16)
            for half in range(2):
                k = slice(half * KT // 2, (half + 1) * KT // 2)
                act.wait_ge(xt_in, 16 * (half + 1))
                nc.scalar.activation(flat(xt_hi[:, 0, k]), flat(xt_raw[:, k]), ACT.Copy).then_inc(xt_hi_cut, 1)
            act.wait_ge(b_in, 16)

            def send(tb, m):
                act.wait_ge(lo_cut, tb * G + (m + 3))
                rows = slice(m * P, (m + 1) * P)
                act.dma_start(q_hi_d[bass.ds(tb, 1), rows].rearrange("a p n -> p (a n)"), part_hi[:, m % 2].bitcast(F32)).then_inc(part_sent[m % 2], 16)
                act.dma_start(q_lo_d[bass.ds(tb, 1), rows].rearrange("a p n -> p (a n)"), part_lo[:, m % 2].bitcast(F32)).then_inc(part_sent[m % 2], 16)

            with act.Fori(0, TB) as tb:
                for m in range(MT):
                    act.wait_ge(qkv_done, tb * MT + (m + 1 + 2 * MT))
                    if m == G:
                        nc.scalar.activation(one(kv[:, bass.ds(tb, 1)]), bank[:, KV_BANK], ACT.Identity, bias=bias[:, m:m + 1]).then_inc(raw_ready, 1)
                    else:
                        u = tb * G + m
                        act.wait_ge(lo_cut, u + 1)
                        nc.scalar.activation(raw[:, m % 2], bank[:, m % 2], ACT.Identity, bias=bias[:, m:m + 1]).then_inc(raw_ready, 1)
                        act.wait_ge(norm_done, u + 1)
                        nc.scalar.activation(sq[:, m % 2], bank[:, m % 2], ACT.Square, bias=bias[:, m:m + 1]).then_inc(sq_ready, 1)
                    if m >= 1:
                        send(tb, m - 1)
            def upper_wo(k):
                act.wait_ge(wo_in[k % 4], 16 * (k // 4 + 1))
                nc.scalar.activation(wo_hi[:, k], wo_stage[:, k % 4], ACT.Copy).then_inc(wo_hi_cut, 1)

            act.wait_ge(qkv_done, (TB + 2) * MT)
            act.dma_start(bo[:], b_o).then_inc(bo_in, 16)
            for k in range(4):
                upper_wo(k)
            act.wait_ge(norm_done, TB * G + 2)
            for tb in range(TB):
                act.wait_ge(centred, tb // JB + 1)
                if tb >= 2:
                    act.wait_ge(k_norm_done, tb - 1)
                nc.scalar.activation(sq[0:HD, tb % 2], kv[0:HD, tb], ACT.Square).then_inc(k_sq, 1)
            act.wait_ge(v_copied, 1)
            act.dma_start(v_d.rearrange("t p q d -> p t (q d)"), v_t[:].rearrange("p t q d -> p t (q d)")).then_inc(kv_sent, 16 * TB)
            for b in range(B):
                act.wait_ge(k_cut, 2 * (b + 1))
                blocks = slice(b * JB, (b + 1) * JB)
                act.dma_start(k_st_d[blocks, 0:2 * HD].rearrange("t r n -> r t n"), k_hi[0:2 * HD, b].bitcast(F32)).then_inc(kv_sent, 16)
                act.dma_start(k_st_d[blocks, 2 * HD:SR].rearrange("t r n -> r t n"), k_lo[b][2 * HD:SR].bitcast(F32)).then_inc(kv_sent, 16)
            for k in range(4, KT):
                upper_wo(k)

            act.wait_ge(flag_ready, 1)
            needed = act.value_load(flag[0:1, 0:1], min_val=0, max_val=1)
            with act.If(needed == 1):
                act.sem_inc(m_sent, 32 * JB)
                with act.Fori(0, B) as b:
                    with act.Fori(0, H) as h:
                        act.wait_ge(m_lo_cut, b * H + h + 2)
                        for c, part in ((0, max_hi), (1, max_lo)):
                            for j in range(JB):
                                act.dma_start(max_d[c].rearrange("t h (q p) -> (t h) q p", p=P)[bass.ds(b * (JB * H) + j * H + h, 1)].rearrange("a q p -> (a q) p"),
                                              part[j * QT:(j + 1) * QT].bitcast(F32)).then_inc(m_sent, 16)

            with act.Fori(0, B) as b:
                act.wait_ge(end_sent, b * (16 * QT) + 16 * QT)
                act.wait_ge(ln1, b * (TT * LN) + LN)

                def body(j, gp, first, last):
                    for r in range(2):
                        s0 = step(b, j, gp, r)
                        for t in range(key_tiles(j)):
                            off = first_query(j, t)
                            act.wait_ge(pv_done, s0 + (t + 1))
                            act.wait_ge(acc_done, s0 + (t + 1))
                            for p in range(2):
                                act.wait_ge(s_done, s0 * 2 + (2 * t + p + 2))
                                nc.scalar.activation(prob[:, t % SLOTS, 2 * p:2 * p + 2, off:NB], bank[:, 2 * p:2 * p + 2, off:NB],
                                                     ACT.Exp, scale=SCALE).then_inc(p_done, 1)
                            if t == 1 and not (first and r == 0):
                                act.wait_ge(pv_done, s0 + SLOTS)
                                nc.scalar.activation(group_before(j, gp, r), bank[:, 4 + (1 - r)], ACT.Copy).then_inc(pv_moved, 1)
                            if j > 0 and r == 0 and t == key_tiles(j) // 2 - 1:
                                act.wait_ge(att_ready, b * SEQ_GROUPS + (j * G + 2))
                                act.wait_ge(y_done, projected(b, j, gp) * 2 + 4)
                                heads = att[:, (j - 1) % 2 * G:(j - 1) % 2 * G + G, bass.ds(gp * P, P)]
                                nc.scalar.activation(att_hi[:], heads, ACT.Copy).then_inc(att_hi_cut, 1)

                pairs_of_groups(act, b, body)
                act.wait_ge(pv_done, (b + 1) * SEQ_STEPS + SLOTS)
                nc.scalar.activation(att[:, (JB - 1) % 2 * G + G - 1], bank[:, 5], ACT.Copy).then_inc(pv_moved, 1)

                def end_store(t):
                    tile = projected(b, JB, t)
                    act.wait_ge(ln1, tile * LN + (LN + 6))
                    act.dma_start(x1_d[bass.ds(tile, 1)].rearrange("a p d -> p (a d)"), end_res[:, t]).then_inc(end_sent, 16)

                for t in range(QT):
                    act.wait_ge(att_ready, b * SEQ_GROUPS + (SEQ_GROUPS + 2))
                    act.wait_ge(y_done, projected(b, JB, t) * 2 + 2)
                    heads = att[:, (JB - 1) % 2 * G:(JB - 1) % 2 * G + G, t * P:(t + 1) * P]
                    nc.scalar.activation(end_hi[:, t % 2], heads, ACT.Copy).then_inc(att_hi_cut, 1)
                    if t >= 2:
                        end_store(t - 2)
                end_store(QT - 2)
                end_store(QT - 1)

            act.wait_ge(y_done, 2 * TILES + 4)
            for k in range(KT):
                act.wait_ge(wf_in[k], 16)
                nc.scalar.activation(wf_hi[:, k], wf[:, k], ACT.Copy).then_inc(wf_hi_cut, 1)

            def upper(r, n):
                act.wait_ge(t_done, n + 3)
                act.wait_ge(f_done, n + 1)
                nc.scalar.activation(xs_hi[:, r % 2].rearrange("p k n -> p (k n)"),
                                     bank[:, 2 * (r % 2):2 * (r % 2) + 2].rearrange("p k n -> p (k n)"), ACT.Copy).then_inc(t_hi, 1)

            def store(r, n):
                act.wait_ge(ln2, n * LN2 + 6)
                act.dma_start(out_tiles[bass.ds(n, 1)].rearrange("a p d -> p (a d)"), y2[:, r % 2]).then_inc(y_sent[r % 2], 16)

            upper(0, 0)
            with act.Fori(0, TILES // 4 - 1) as i:
                for r in range(4):
                    upper(r + 1, i * 4 + r + 1)
                    store(r, i * 4 + r)
            i = TILES // 4 - 1
            for r in range(4):
                if r < 3:
                    upper(r + 1, i * 4 + r + 1)
                store(r, i * 4 + r)

        @block.vector
        def _(dve):
            def moments_of(z, stats, moments, done, before):
                for h in range(NH):
                    nc.vector.bn_stats(stats[:, h], z[:, h * 512:(h + 1) * 512]).then_inc(done, 1)
                wait_apart(dve, done, before + NH)
                nc.vector.bn_aggr(moments[:, 0:2], stats[:]).then_inc(done, 1)

            def normalise(z, moments, done, before):
                dve.wait_ge(done, before + (NH + 3))
                nc.vector.tensor_scalar(z, z, moments[:, 0:1], moments[:, 2:3], ALU.subtract, ALU.mult).then_inc(done, 1)

            dve.sem_inc(wf_tile_read, 1)
            dve.sem_inc(norm_read, 2)
            dve.sem_inc(lo_cut, 2)
            dve.sem_inc(acc_done, SLOTS)
            dve.sem_inc(att_ready, 2)
            dve.sem_inc(y_read, 2)
            dve.sem_inc(ln1, LN)
            dve.sem_inc(t_lo, 2)
            dve.sem_inc(f_read, 4)
            def lower_x(half):
                k = slice(half * KT // 2, (half + 1) * KT // 2)
                dve.wait_ge(xt_hi_cut, half + 1)
                nc.vector.tensor_tensor(xt_lo[0][:, k], xt_raw[:, k], xt_hi[:, 0, k].bitcast(F32), ALU.subtract).then_inc(xt_cut, 1)

            for m in range(MT):
                if m == 1:
                    lower_x(0)
                    lower_x(1)
                dve.wait_ge(w_in[m % 2], 16 * (m // 2 + 1))
                nc.vector.tensor_copy(w_hi[:, m], w_stage[:, m % 2]).then_inc(w_hi_cut, 1)
                dve.wait_ge(w_hi_cut, m + 1)
                nc.vector.tensor_tensor(w_lo[:, m], w_stage[:, m % 2], w_hi[:, m].bitcast(F32), ALU.subtract).then_inc(w_cut, 1)

            def norm(tb, m):
                dve.wait_ge(norm_done, tb * G + (m + 3))
                nc.vector.reduce_max(norms[:, bass.ds(tb, 1), m:m + 1].rearrange("p a b -> p (a b)"), bank[:, 2 + m % 2], AX.X).then_inc(norm_read, 1)

            with dve.Fori(0, TB) as tb:
                for m in range(G):
                    u = tb * G + m
                    dve.wait_ge(raw_ready, tb * MT + (m + 3))
                    dve.wait_ge(part_sent[m % 2], tb * (16 * G) + 32 * (m // 2 + 1))
                    nc.vector.tensor_copy(part_hi[:, m % 2], raw[:, m % 2]).then_inc(hi_cut, 1)
                    dve.wait_ge(hi_cut, u + 1)
                    nc.vector.tensor_tensor(part_lo[:, m % 2], raw[:, m % 2], part_hi[:, m % 2].bitcast(F32), ALU.subtract).then_inc(lo_cut, 1)
                    if m >= 1:
                        norm(tb, m - 1)
                    if m == 1:
                        dve.wait_ge(wf_tile_in, tb * 16 + 16)
                        nc.vector.tensor_reduce(amax_w[:, bass.ds(tb, 1)], wf_tile[:], AX.X, ALU.max, apply_absolute_value=True).then_inc(wf_tile_read, 1)
                norm(tb, G - 1)

                dve.wait_ge(raw_ready, tb * MT + (MT + 2))
                nc.vector.reduce_sum(centre_part[0:SR, bass.ds(tb, 1)], one(kv[0:SR, bass.ds(tb, 1)]), AX.X).then_inc(k_summed, 1)

            for b in range(B):
                keys = kv[0:SR, b * JB:(b + 1) * JB]
                dve.wait_ge(k_summed, TB + 2 * b)
                nc.vector.reduce_sum(centre[0:SR, b:b + 1], centre_part[0:SR, b * JB:(b + 1) * JB], AX.X).then_inc(k_summed, 1)
                dve.wait_ge(k_summed, TB + 2 * b + 1)
                nc.vector.tensor_scalar(centre[0:SR, b:b + 1], centre[0:SR, b:b + 1], 1.0 / T, None, ALU.mult).then_inc(k_summed, 1)
                dve.wait_ge(k_summed, TB + 2 * b + 2)
                nc.vector.tensor_scalar(keys, keys, centre[0:SR, b:b + 1], None, ALU.subtract).then_inc(centred, 1)
            dve.wait_ge(v_turned, 1)
            nc.vector.tensor_copy(v_t[:].rearrange("p t q d -> p (t q d)"), bank[:, 0:2].rearrange("p a n -> p (a n)")).then_inc(v_copied, 1)
            for b in range(B):
                keys = kv[0:SR, b * JB:(b + 1) * JB]
                dve.wait_ge(centred, b + 1)
                nc.vector.tensor_copy(k_hi[0:SR, b], keys).then_inc(k_cut, 1)
                dve.wait_ge(k_cut, 2 * b + 1)
                nc.vector.tensor_tensor(k_lo[b][0:SR], keys, k_hi[0:SR, b].bitcast(F32), ALU.subtract).then_inc(k_cut, 1)
            for tb in range(TB):
                dve.wait_ge(k_norm_done, tb + 1)
                nc.vector.reduce_max(norms[:, tb, G:MT], bank[:, 2 + tb % 2], AX.X).then_inc(k_norm_read, 1)

            dve.wait_ge(norm_read, TB * G + 2)
            dve.wait_ge(k_norm_read, TB)
            dve.wait_ge(wf_tile_read, KT + 1)
            nc.vector.memset(small[:, 0:3], 0.0).then_inc(bound_steps, 1)
            dve.wait_ge(bound_steps, 1)
            nc.vector.tensor_reduce(small[:, 0:1], norms[:, :, 0:G], AX.XY, ALU.max).then_inc(bound_steps, 1)
            nc.vector.tensor_reduce(small[0:HD, 1:2], one(norms[0:HD, :, G:MT]), AX.X, ALU.max).then_inc(bound_steps, 1)
            nc.vector.tensor_reduce(small[:, 2:3], amax_w[:], AX.X, ALU.max).then_inc(bound_steps, 1)
            dve.wait_ge(bound_all, 1)
            nc.vector.tensor_tensor(small[:, 6:7], small[:, 3:4], small[:, 4:5], ALU.mult).then_inc(bound_steps, 1)
            dve.wait_ge(bound_steps, 5)
            nc.vector.tensor_scalar(flag[:], small[:, 6:7], SAFE_NORMS, None, ALU.is_gt).then_inc(flag_ready, 1)
            nc.vector.tensor_scalar(small[:, 13:14], small[:, 5:6], SCALE_EPS, None, ALU.max).then_inc(bound_steps, 1)
            dve.wait_ge(bound_steps, 6)
            nc.vector.reciprocal(small[:, 17:18], small[:, 13:14]).then_inc(bound_steps, 1)
            dve.wait_ge(bound_steps, 7)
            nc.vector.tensor_scalar(small[:, 15:16], small[:, 17:18], FP8_MAX, None, ALU.mult).then_inc(bound_steps, 1)
            dve.wait_ge(wo_cut, KT // 2)
            for k in range(KT // 2, KT):
                dve.wait_ge(wo_hi_cut, k + 1)
                nc.vector.tensor_tensor(wo_lo[:, k], wo_stage[:, k % 4], wo_hi[:, k].bitcast(F32), ALU.subtract).then_inc(wo_cut, 1)

            dve.wait_ge(flag_ready, 1)
            needed = dve.value_load(flag[0:1, 0:1], min_val=0, max_val=1)
            with dve.If(needed == 1):
                dve.sem_inc(m_s_read, 2)
                dve.sem_inc(m_lo_cut, 1)
                dve.wait_ge(project_over, 1)
                with dve.Fori(0, B) as b:
                    with dve.Fori(0, H) as h:
                        n = b * H + h
                        for q in range(TT):
                            scores = bank[:, 4 * (q % 2):4 * (q % 2) + 4].rearrange("p a n -> p (a n)")[:, 0:(q + 1) * P]
                            dve.wait_ge(m_s_done, n * TT + (q + 1))
                            nc.vector.reduce_max(row_max[:, q:q + 1], scores, AX.X).then_inc(m_s_read, 1)
                        dve.wait_ge(m_turned, n + 3)
                        dve.wait_ge(m_sent, n * (32 * JB) + 32 * JB)
                        nc.vector.tensor_copy(max_hi[:], bank[0:TT, 0, 0:P]).then_inc(m_hi_cut, 1)
                        dve.wait_ge(m_hi_cut, n + 1)
                        nc.vector.tensor_tensor(max_lo[:], bank[0:TT, 0, 0:P], max_hi[:].bitcast(F32), ALU.subtract).then_inc(m_lo_cut, 1)

            def invert(n):
                dve.wait_ge(den_done, n + 3)
                nc.vector.reciprocal(r_den[:], bank[:, DEN_BANK, 0:P]).then_inc(den_read, 1)

            def normalise_group(n, slot):
                dve.wait_ge(spread_done, n + 1)
                dve.wait_ge(pv_moved, n + 3)
                nc.vector.tensor_tensor(slot, slot, bank[:, DEN_BANK], ALU.mult).then_inc(att_ready, 1)

            def add_residual(z, tile, half, y_bank):
                cols = slice(half * 512, (half + 1) * 512)
                dve.wait_ge(y_done, tile * 2 + (half + 5))
                dve.wait_ge(res_ready, tile + 1)
                nc.vector.tensor_tensor(z[:, cols], bank[:, y_bank], z[:, cols], ALU.add).then_inc(y_read, 1)

            def largest(z, tile):
                dve.wait_ge(ln1, tile * LN + (LN + 6))
                nc.vector.tensor_reduce(amax_x[:, bass.ds(tile, 1)], z, AX.X, ALU.max, apply_absolute_value=True).then_inc(ln1, 1)

            with dve.Fori(0, B) as b:
                def body(j, gp, first, last):
                    for r in range(2):
                        n, s0 = group(b, j, gp, r), step(b, j, gp, r)
                        NT = key_tiles(j)
                        dve.wait_ge(den_done, n + 1)
                        for t in range(NT):
                            off = first_query(j, t)
                            if t >= 1:
                                dve.wait_ge(p_done, s0 * 2 + (2 * t + 4))
                                if t >= QT * j:
                                    dve.wait_ge(masked, n * QT + (t - QT * j + 1))
                                new = prob[:, t % SLOTS, :, off:NB]
                                if t == 1:
                                    if off > 0:
                                        nc.vector.tensor_copy(acc[:, r, :, 0:off], prob[:, 0, :, 0:off])
                                    nc.vector.tensor_tensor(acc[:, r, :, off:NB], prob[:, 0, :, off:NB], new, ALU.add).then_inc(acc_done, 2)
                                else:
                                    dve.wait_ge(acc_done, s0 + (t + SLOTS))
                                    nc.vector.tensor_tensor(acc[:, r, :, off:NB], acc[:, r, :, off:NB], new, ALU.add).then_inc(acc_done, 1)
                            if t == 2 and not (first and r == 0):
                                invert(n - 1)
                            if t == 3 and not (first and r == 0):
                                normalise_group(n - 1, group_before(j, gp, r))
                            if j == 0 and r == 0 and t == 2:
                                piece = b * (G // 2) + gp
                                dve.wait_ge(piece_in, piece * 16 + 16)
                                nc.vector.tensor_scalar(wf_piece[:], wf_piece[:], small[:, 15:16], FP8_MAX, ALU.mult, ALU.min).then_inc(piece_clip, 1)
                                dve.wait_ge(piece_clip, piece * 2 + 1)
                                nc.vector.tensor_scalar(wf_piece[:], wf_piece[:], -FP8_MAX, None, ALU.max).then_inc(piece_clip, 1)
                            if j > 0:
                                tile = projected(b, j, gp)
                                if r == 1 and t == 1:
                                    add_residual(res[:], tile, 0, Y_BANK)
                                if r == 1 and t == min(NT // 2 + 4, NT - 1):
                                    add_residual(res[:], tile, 1, Y_BANK)
                                    dve.wait_ge(y_read, tile * 2 + 4)
                                    moments_of(res[:], stats[:, 0], moments[:, 0], ln1, tile * LN + LN)
                                if r == 1 and t == NT - 1:
                                    normalise(res[:], moments[:, 0], ln1, tile * LN + LN)
                                    largest(res[:], tile)

                pairs_of_groups(dve, b, body)
                invert(b * SEQ_GROUPS + (SEQ_GROUPS - 1))
                normalise_group(b * SEQ_GROUPS + (SEQ_GROUPS - 1), att[:, (JB - 1) % 2 * G + G - 1])

                def end_normalise(t):
                    tile = projected(b, JB, t)
                    normalise(end_res[:, t], moments[:, t % 2], ln1, tile * LN + LN)
                    largest(end_res[:, t], tile)

                for t in range(QT):
                    tile = projected(b, JB, t)
                    for half in range(2):
                        add_residual(end_res[:, t], tile, half, Y_BANK - half)
                    dve.wait_ge(y_read, tile * 2 + 4)
                    if t >= 1:
                        end_normalise(t - 1)
                    moments_of(end_res[:, t], stats[:, t % 2], moments[:, t % 2], ln1, tile * LN + LN)
                end_normalise(QT - 1)

            dve.wait_ge(ln1, LN * (TILES + 1))
            nc.vector.tensor_reduce(small[:, 8:9], amax_x[:], AX.X, ALU.max).then_inc(scale_steps, 1)
            dve.wait_ge(g_all, 1)
            nc.vector.tensor_scalar(small[:, 12:13], small[:, 9:10], SCALE_EPS, None, ALU.max).then_inc(scale_steps, 1)
            dve.wait_ge(scale_steps, 2)
            nc.vector.reciprocal(small[:, 16:17], small[:, 12:13]).then_inc(scale_steps, 1)
            dve.wait_ge(scale_steps, 3)
            nc.vector.tensor_scalar(small[:, 14:15], small[:, 16:17], FP8_MAX, None, ALU.mult).then_inc(scale_steps, 1)
            dve.wait_ge(scale_steps, 4)
            dve.wait_ge(x1_in[0], 16)
            nc.vector.tensor_scalar(x_sim[:, 0], x1[:, 0], small[:, 14:15], FP8_MAX, ALU.mult, ALU.min).then_inc(sim_ready, 1)
            dve.wait_ge(sim_ready, 1)
            nc.vector.tensor_scalar(x_sim[:, 0], x_sim[:, 0], -FP8_MAX, None, ALU.max).then_inc(sim_ready, 1)
            nc.vector.tensor_tensor(small[:, 18:19], small[:, 14:15], small[:, 15:16], ALU.mult).then_inc(scale_steps, 1)
            dve.wait_ge(scale_steps, 5)
            nc.vector.reciprocal(small[:, 19:20], small[:, 18:19]).then_inc(scale_steps, 1)

            def lower_wf(k):
                dve.wait_ge(wf_hi_cut, k + 1)
                nc.vector.tensor_tensor(wf_lo[:, k], wf[:, k], wf_hi[:, k].bitcast(F32), ALU.subtract).then_inc(wf_cut, 1)

            def lower(r, n):
                dve.wait_ge(t_hi, n + 1)
                dve.wait_ge(f_done, n + 1)
                nc.vector.tensor_tensor(xs_lo[:, r % 2].rearrange("p k n -> p (k n)"),
                                        bank[:, 2 * (r % 2):2 * (r % 2) + 2].rearrange("p k n -> p (k n)"),
                                        xs_hi[:, r % 2].rearrange("p k n -> p (k n)").bitcast(F32), ALU.subtract).then_inc(t_lo, 1)

            def finish(i, r, n):
                s = r % 2
                z = y2[:, s]
                dve.wait_ge(f_done, n + 3)
                dve.wait_ge(y_sent[s], i * 32 + 16 * (r // 2 + 1))
                nc.vector.scalar_tensor_tensor(out=z, in0=bank[:, 4 + 2 * s:4 + 2 * s + NH].rearrange("p a n -> p (a n)"), scalar=small[:, 19:20],
                                               in1=x1[:, r], op0=ALU.mult, op1=ALU.add).then_inc(f_read, 1)
                dve.wait_ge(f_read, n + 5)
                moments_of(z, stats2[:, s], moments2[:, s], ln2, n * LN2)
                normalise(z, moments2[:, s], ln2, n * LN2)

            for k in range(2):
                lower_wf(k)
            lower(0, 0)
            for k in range(2, KT):
                lower_wf(k)
            dve.wait_ge(end_sent, 16 * QT * (B + 1))
            with dve.Fori(0, TILES // 4 - 1) as i:
                for r in range(4):
                    lower(r + 1, i * 4 + r + 1)
                    finish(i, r, i * 4 + r)
            i = TILES // 4 - 1
            for r in range(4):
                if r < 3:
                    lower(r + 1, i * 4 + r + 1)
                finish(i, r, i * 4 + r)

        @block.tensor
        def _(pe):
            THREE = ((0, 0), (1, 0), (0, 1))

            pe.sem_inc(qkv_done, 2 * MT)
            pe.sem_inc(norm_done, 2)
            pe.sem_inc(s_done, 1)
            pe.sem_inc(pv_done, SLOTS)
            pe.sem_inc(den_done, 2)
            pe.sem_inc(y_done, 4)
            pe.sem_inc(t_done, 2)
            pe.sem_inc(f_done, 2)
            pe.wait_ge(consts, 8 + HG)

            def norm(tb, m):
                pe.wait_ge(sq_ready, tb * G + (m + 3))
                pe.wait_ge(norm_read, tb * G + (m + 1))
                nc.tensor.matmul(bank[:, 2 + m % 2], head_sum[:], sq[:, m % 2], start=True, stop=True).then_inc(norm_done, 1)

            with pe.Fori(0, TB // 2) as i:
                for r in range(2):
                    tb = i * 2 + r
                    for m in range(MT):
                        pe.wait_ge(w_cut, m + 1)
                        if m < G:
                            pe.wait_ge(sq_ready, tb * G + (m + 1))
                        else:
                            pe.wait_ge(raw_ready, tb * MT + 2)
                        dst = bank[:, m % 2 if m < G else KV_BANK]
                        for k in range(KT):
                            if m == 0 and k % (KT // 2) == 0:
                                pe.wait_ge(xt_cut, tb * 2 + (2 + k // (KT // 2) + 1))
                            for a, c in THREE:
                                last = nc.tensor.matmul(dst, (w_hi, w_lo)[a][:, m, k], (xt_hi[:, r], xt_lo[r])[c][:, k],
                                                        start=(k == 0 and a == c == 0), stop=(k == KT - 1 and c == 1))
                        last.then_inc(qkv_done, 1)
                        if m >= 1:
                            norm(tb, m - 1)
            pe.wait_ge(raw_ready, TB * MT + 2)
            pe.wait_ge(sq_ready, TB * G + 2)
            for tt in range(TILES):
                tb, q = tt // QT, tt % QT
                last = nc.tensor.transpose(bank[:, tt // (TILES // 2), tt % (TILES // 2) * HD:(tt % (TILES // 2) + 1) * HD],
                                           kv[SR:P, tb, q * P:(q + 1) * P], ident[SR:P, SR:P])
            last.then_inc(v_turned, 1)
            pe.wait_ge(norm_read, TB * G + 2)
            for tb in range(TB):
                pe.wait_ge(k_sq, tb + 1)
                if tb >= 2:
                    pe.wait_ge(k_norm_read, tb - 1)
                nc.tensor.matmul(bank[:, 2 + tb % 2], head_sum[0:HD, :], sq[0:HD, tb % 2], start=True, stop=True).then_inc(k_norm_done, 1)

            pe.wait_ge(flag_ready, 1)
            needed = pe.value_load(flag[0:1, 0:1], min_val=0, max_val=1)
            with pe.If(needed == 1):
                pe.sem_inc(m_turned, 2)
                with pe.Fori(0, B) as b:
                    wait_apart(pe, m_k_in, b * 16 + 16)
                    with pe.Fori(0, H // 2) as hp:
                        for r in range(2):
                            n = b * H + r + hp * 2
                            pe.wait_ge(m_q_in[r], b * (48 * H // 2) + hp * 48 + 48)
                            for q in range(TT):
                                pe.wait_ge(m_s_read, n * TT + (q + 1))
                                if q == 0:
                                    pe.wait_ge(m_lo_cut, n + 1)
                                queries = q_m[:, r, q * P:(q + 1) * P]
                                for c in range(q // 4 + 1):
                                    own = c == q // 4
                                    width = (q % 4 + 1) * P if own else 512
                                    dst = bank[:, 4 * (q % 2) + c]
                                    nc.tensor.matmul(dst[:, 0:width], queries, k_m[:, c * 512:c * 512 + width], start=True, stop=not own)
                                    if own:
                                        last = nc.tensor.matmul(dst[:, width - P:width], ident_bf[:], mask_bf[:], start=False, stop=True)
                                last.then_inc(m_s_done, 1)
                            pe.wait_ge(m_s_read, n * TT + (TT + 2))
                            nc.tensor.transpose(bank[0:TT, 0, 0:P], row_max[:], ident[:]).then_inc(m_turned, 1)

            pe.wait_ge(fixed, FIXED)

            def half_projection(hi, lo, half, y_bank, part, parts):
                todo = [(k, a, c) for k in range(KT) for a, c in THREE]
                cols = slice(half * 512, (half + 1) * 512)
                for i in range(len(todo) * part // parts, len(todo) * (part + 1) // parts):
                    k, a, c = todo[i]
                    last = nc.tensor.matmul(bank[:, y_bank], (hi, lo)[a][:, k], (wo_hi, wo_lo)[c][:, k, cols],
                                            start=(i == 0), stop=(i == len(todo) - 1), skip_group_check=True)
                if part == parts - 1:
                    last.then_inc(y_done, 1)

            with pe.Fori(0, B) as b:
                def scores(s0, j, slot, t):
                    off = first_query(j, t)
                    for p in range(2):
                        pe.wait_ge(p_done, s0 * 2 + (2 * t + p + 1))
                        for h in (2 * p, 2 * p + 1):
                            last = nc.tensor.matmul(bank[:, h, off:NB], k_st[:, t * P:(t + 1) * P], q_st[:, slot, h, off:NB], start=True, stop=True)
                        last.then_inc(s_done, 1)

                def denominators(n, r):
                    pe.wait_ge(att_ready, n + 2)
                    for h in range(HG):
                        for c in range(QT):
                            last = nc.tensor.matmul(bank[c * HD:(c + 1) * HD, DEN_BANK, 0:P], head_col[:, h], acc[:, r, h, c * P:(c + 1) * P],
                                                    start=(h == 0), stop=(h == HG - 1), skip_group_check=True)
                    last.then_inc(den_done, 1)

                def spread_out(n):
                    pe.wait_ge(den_read, n + 1)
                    for c in range(QT):
                        last = nc.tensor.matmul(bank[:, DEN_BANK, c * P:(c + 1) * P], spread[:, c], r_den[:], start=True, stop=True)
                    last.then_inc(spread_done, 1)

                wait_apart(pe, kv_in, b * 32 + 32)
                pe.wait_ge(q_in, b * (SEQ_GROUPS * 64) + 64)
                scores(b * SEQ_STEPS, 0, 0, 0)

                def body(j, gp, first, last_pair):
                    NT = key_tiles(j)
                    for r in range(2):
                        n, s0 = group(b, j, gp, r), step(b, j, gp, r)
                        for t in range(NT):
                            if t + 1 < NT:
                                scores(s0, j, r, t + 1)
                            elif not (last_pair and r == 1):
                                pe.wait_ge(q_in, n * 64 + 128)
                                scores(s0 + NT, 0, 1 - r, 0)
                            off = first_query(j, t)
                            if t == 0:
                                pe.wait_ge(pv_moved, n + 1)
                            pe.wait_ge(p_done, s0 * 2 + (2 * t + 4))
                            if t >= QT * j:
                                pe.wait_ge(masked, n * QT + (t - QT * j + 1))
                            for h in range(HG):
                                last = nc.tensor.matmul(bank[h * HD:(h + 1) * HD, 4 + r, off:NB], v_sb[:, t], prob[:, t % SLOTS, h, off:NB],
                                                        start=(t == 0), stop=(t == NT - 1), skip_group_check=True)
                            last.then_inc(pv_done, 1)
                            if t == 1 and not (first and r == 0):
                                pe.wait_ge(acc_done, s0 + SLOTS)
                                denominators(n - 1, 1 - r)
                            if t == 3 and not (first and r == 0):
                                spread_out(n - 1)
                            if j > 0 and t in (window := projection_steps(j, r)):
                                if t == window[0]:
                                    tile = projected(b, j, gp)
                                    pe.wait_ge(att_cut, tile + 1)
                                    pe.wait_ge(y_read, tile * 2 + (r + 2))
                                half_projection(att_hi, att_lo, r, Y_BANK, t - window[0], len(window))

                pairs_of_groups(pe, b, body)
                pe.wait_ge(acc_done, (b + 1) * SEQ_STEPS + SLOTS)
                denominators(b * SEQ_GROUPS + (SEQ_GROUPS - 1), 1)
                spread_out(b * SEQ_GROUPS + (SEQ_GROUPS - 1))
                for t in range(QT):
                    tile = projected(b, JB, t)
                    pe.wait_ge(att_cut, tile + 1)
                    for half in range(2):
                        if t == 0 and half == 0:
                            pe.wait_ge(y_read, tile * 2 + 2)
                            pe.wait_ge(att_ready, b * SEQ_GROUPS + (SEQ_GROUPS + 2))
                        elif t >= 1:
                            pe.wait_ge(y_read, tile * 2 + (half + 1))
                        half_projection(end_hi[:, t % 2], end_lo[:, t % 2], half, Y_BANK - half, 0, 1)

            def turn(r, n):
                pe.wait_ge(sim_ready, n * 2 + 2)
                pe.wait_ge(t_lo, n + 1)
                for k in range(KT):
                    last = nc.tensor.transpose(bank[:, 2 * (r % 2) + k // 4, (k % 4) * P:(k % 4 + 1) * P], x_sim[:, r % 2, k * P:(k + 1) * P], ident[:])
                last.then_inc(t_done, 1)

            def product(r, n):
                pe.wait_ge(t_lo, n + 3)
                pe.wait_ge(f_read, n + 3)
                for h in range(NH):
                    cols = slice(h * 512, (h + 1) * 512)
                    for k in range(KT):
                        pe.wait_ge(wf_cut, k + 1)
                        for a, c in THREE:
                            last = nc.tensor.matmul(bank[:, 4 + 2 * (r % 2) + h], (xs_hi, xs_lo)[a][:, r % 2, k], (wf_hi, wf_lo)[c][:, k, cols],
                                                    start=(k == 0 and a == c == 0), stop=(k == KT - 1 and c == 1))
                last.then_inc(f_done, 1)

            pe.wait_ge(y_read, 2 * TILES + 2)
            turn(0, 0)
            with pe.Fori(0, TILES // 4 - 1) as i:
                for r in range(4):
                    turn(r + 1, i * 4 + r + 1)
                    product(r, i * 4 + r)
            i = TILES // 4 - 1
            for r in range(4):
                if r < 3:
                    turn(r + 1, i * 4 + r + 1)
                product(r, i * 4 + r)

    return nc


HEADS = 32


def kernel(L0_attn_x, L0_attn_wq_w, L0_attn_wq_b, L0_attn_wk_w, L0_attn_wk_b, L0_attn_wv_w, L0_attn_wv_b,
           L0_attn_wo_w, L0_attn_wo_b, L0_ffn_weight):
    import numpy as np
    import concourse.bacc as bacc
    from concourse.bass_utils import run_bass_kernel_spmd

    x = np.ascontiguousarray(L0_attn_x)
    B, T, D = x.shape
    kt = D // P

    def by_partition(w):
        return np.ascontiguousarray(w.reshape(kt, P, -1).transpose(1, 0, 2))

    flat = x.reshape(B * T, D)
    blocks = flat.reshape(-1, 512, kt, P).transpose(0, 3, 2, 1)
    w_qkv = np.concatenate([np.asarray(w) for w in (L0_attn_wq_w, L0_attn_wk_w, L0_attn_wk_w, L0_attn_wk_w, L0_attn_wv_w)]).T
    b_qkv = np.concatenate([np.asarray(w) for w in (L0_attn_wq_b, L0_attn_wk_b, L0_attn_wk_b, L0_attn_wk_b, L0_attn_wv_b)])
    arrays = {
        "x_t": np.ascontiguousarray(blocks),
        "x": flat,
        "w_qkv": np.ascontiguousarray(w_qkv.reshape(kt, P, -1, P).transpose(1, 2, 0, 3)),
        "b_qkv": np.ascontiguousarray(b_qkv.reshape(-1, P).T),
        "w_o": by_partition(np.asarray(L0_attn_wo_w).T),
        "b_o": np.ascontiguousarray(np.broadcast_to(np.asarray(L0_attn_wo_b), (P, D))),
        "w_f": by_partition(np.asarray(L0_ffn_weight)),
    }
    nc = bacc.Bacc("TRN2", target_bir_lowering=False, num_devices=1)
    aps = {n: nc.dram_tensor(n, a.shape, mybir.dt.from_np(a.dtype), kind="ExternalInput").ap() for n, a in arrays.items()}
    out = nc.dram_tensor("out", (B * T, D), F32, kind="ExternalOutput").ap()
    build(nc, out=out, B=B, T=T, H=HEADS, **aps)
    r = run_bass_kernel_spmd(nc, [arrays], core_ids=[0])
    return r.results[0]["out"].reshape(B, T, D)
```
